# Optimizing a Trainium2 kernel written in Bass

```python
import numpy as np
import jax
import jax.numpy as jnp

def _softmax(x, axis=-1):
    return jax.nn.softmax(x, axis=axis)

def _gelu(x):
    return jax.nn.gelu(x, approximate=True)

def _silu(x):
    return jax.nn.silu(x)

def _sigmoid(x):
    return jax.nn.sigmoid(x)

def _layernorm(x, axis=-1, eps=1e-05):
    m = jnp.mean(x, axis=axis, keepdims=True)
    v = jnp.var(x, axis=axis, keepdims=True)
    return (x - m) / jnp.sqrt(v + eps)

def _scatter_add(tgt, idx, src, axis=0):
    return tgt.at[idx].add(src)

def _segment_sum(src, seg, n):
    return jax.ops.segment_sum(src, seg, n)
kernel_name = 'mk_recurrent_d1_jaxref_r4_0bd0a1'

def setup_inputs(seed: int=0):
    np.random.seed(seed)
    _w = jnp.asarray

    def _L0_attn_setup():
        import jax, jax.numpy as jnp
        import numpy as np
        B, C, L = (64, 128, 1024)
        key = jax.random.key(seed)
        x = jax.random.normal(key, (B, C, L), dtype=jnp.float32)
        return {'x': x}
    _L0_attn_in = _L0_attn_setup()

    def _L0_ffn_setup():
        import jax, jax.numpy as jnp
        import numpy as np
        NF4 = jnp.array([-1.0, -0.6961928009986877, -0.5250730514526367, -0.39491748809814453, -0.28444138169288635, -0.18477343022823334, -0.09105003625154495, 0.0, 0.07958029955625534, 0.16093020141124725, 0.24611230194568634, 0.33791524171829224, 0.44070982933044434, 0.5626170039176941, 0.7229568362236023, 1.0], dtype=jnp.float32)
        BLOCK = 64

        def dequant_nf4(codes, scales):
            out_dim, in_dim = codes.shape
            vals = NF4[codes].reshape(out_dim, in_dim // BLOCK, BLOCK)
            return (vals * scales[:, :, None]).reshape(out_dim, in_dim)
        key = jax.random.key(seed)
        ks = jax.random.split(key, 7)
        H, I = (1024, 2752)
        B, S = (4, 512)
        return {'x': jax.random.normal(ks[0], (B, S, H), dtype=jnp.float32), 'gate_codes': jax.random.randint(ks[1], (I, H), 0, 16, dtype=jnp.int32), 'gate_scales': jax.random.uniform(ks[2], (I, H // BLOCK), dtype=jnp.float32) * 0.02, 'up_codes': jax.random.randint(ks[3], (I, H), 0, 16, dtype=jnp.int32), 'up_scales': jax.random.uniform(ks[4], (I, H // BLOCK), dtype=jnp.float32) * 0.02, 'down_codes': jax.random.randint(ks[5], (H, I), 0, 16, dtype=jnp.int32), 'down_scales': jax.random.uniform(ks[6], (H, I // BLOCK), dtype=jnp.float32) * 0.02}
    _L0_ffn_in = _L0_ffn_setup()
    _d = {'L0_attn_x': _L0_attn_in['x'], 'L0_ffn_gate_codes': _L0_ffn_in['gate_codes'], 'L0_ffn_gate_scales': _L0_ffn_in['gate_scales'], 'L0_ffn_up_codes': _L0_ffn_in['up_codes'], 'L0_ffn_up_scales': _L0_ffn_in['up_scales'], 'L0_ffn_down_codes': _L0_ffn_in['down_codes'], 'L0_ffn_down_scales': _L0_ffn_in['down_scales']}
    _x0 = _d['L0_attn_x']
    _d['L0_attn_x'] = jax.random.normal(jax.random.fold_in(jax.random.key(seed), 1), (4, 1024, 1024), dtype=_x0.dtype)
    del _x0
    return _d

def reference(L0_attn_x, L0_ffn_gate_codes, L0_ffn_gate_scales, L0_ffn_up_codes, L0_ffn_up_scales, L0_ffn_down_codes, L0_ffn_down_scales):

    def _L0_attn_ref(x):
        import jax, jax.numpy as jnp
        import numpy as np
        B, C, L = (64, 128, 1024)
        b, c, l = x.shape
        q = jnp.transpose(x, (2, 0, 1))
        scale = jnp.asarray(c, x.dtype) ** 0.5
        scores = jnp.einsum('lnc,lmc->lnm', q, q) / scale
        prob = jax.nn.softmax(scores, axis=-1)
        msg = jnp.einsum('lnm,lmc->lnc', prob, q)
        return x + jnp.transpose(msg, (1, 2, 0))

    def _L0_ffn_ref(x, gate_codes, gate_scales, up_codes, up_scales, down_codes, down_scales):
        import jax, jax.numpy as jnp
        import numpy as np
        NF4 = jnp.array([-1.0, -0.6961928009986877, -0.5250730514526367, -0.39491748809814453, -0.28444138169288635, -0.18477343022823334, -0.09105003625154495, 0.0, 0.07958029955625534, 0.16093020141124725, 0.24611230194568634, 0.33791524171829224, 0.44070982933044434, 0.5626170039176941, 0.7229568362236023, 1.0], dtype=jnp.float32)
        BLOCK = 64

        def dequant_nf4(codes, scales):
            out_dim, in_dim = codes.shape
            vals = NF4[codes].reshape(out_dim, in_dim // BLOCK, BLOCK)
            return (vals * scales[:, :, None]).reshape(out_dim, in_dim)
        Wg = dequant_nf4(gate_codes, gate_scales)
        Wu = dequant_nf4(up_codes, up_scales)
        Wd = dequant_nf4(down_codes, down_scales)
        gate = jnp.einsum('bsh,ih->bsi', x, Wg)
        up = jnp.einsum('bsh,ih->bsi', x, Wu)
        inter = jax.nn.silu(gate) * up
        return jnp.einsum('bsi,hi->bsh', inter, Wd)
    x = L0_attn_x
    xn = _layernorm(x, axis=-1)
    s = _L0_attn_ref(xn)
    g = _silu(_L0_ffn_ref(xn, L0_ffn_gate_codes, L0_ffn_gate_scales, L0_ffn_up_codes, L0_ffn_up_scales, L0_ffn_down_codes, L0_ffn_down_scales))
    x = x + s * g
    return x

_drawn_inputs = setup_inputs


def setup_inputs(seed=0):
    import zlib

    import numpy as np

    out = dict(_drawn_inputs(seed))
    spreads = {}
    factors = {'L0_ffn_gate_scales': 8.0, 'L0_ffn_up_scales': 8.0, 'L0_ffn_down_scales': 8.0}
    for name, (base, spread) in spreads.items():
        noise = np.random.default_rng([zlib.crc32(name.encode()), seed]).standard_normal(out[name].shape)
        drawn = base * np.exp(spread * noise) if base else spread * noise
        out[name] = jnp.asarray(drawn.astype(out[name].dtype))
    for name, factor in factors.items():
        out[name] = (out[name] * factor).astype(out[name].dtype)
    return out
```

```python
from contextlib import ExitStack

import numpy as np
import concourse.bass as bass
from concourse import mybir

ALU = mybir.AluOpType
ACT = mybir.ActivationFunctionType
AX = mybir.AxisListType
F32 = mybir.dt.float32
F16 = mybir.dt.float16
BF16 = mybir.dt.bfloat16
I32 = mybir.dt.int32
RMAX = bass.bass_isa.ReduceOp.max

P = 128
EPS = 1e-5

NF4 = [-1.0, -0.6961928009986877, -0.5250730514526367, -0.39491748809814453, -0.28444138169288635,
       -0.18477343022823334, -0.09105003625154495, 0.0, 0.07958029955625534, 0.16093020141124725,
       0.24611230194568634, 0.33791524171829224, 0.44070982933044434, 0.5626170039176941, 0.7229568362236023, 1.0]


def nf4_lines():
    f = np.float32

    def near(v, n):
        v = f(v)
        out, up, down = [v], v, v
        for _ in range(n):
            up, down = np.nextafter(up, f(9)), np.nextafter(down, f(-9))
            out += [up, down]
        return out

    def line(k, sign):
        v0, v1 = f(sign * NF4[k]), f(sign * NF4[k + 1])
        slope = float(v1) - float(v0)
        offset = float(v0) - slope * (k - 7)
        for a in near(slope, 8):
            for b in near(offset, 24):
                if (f(np.float64(a) * (k - 7) + np.float64(b)) == v0
                        and f(np.float64(a) * (k - 6) + np.float64(b)) == v1):
                    return float(a), float(b)
        raise AssertionError(k)

    return [line(k, 1.0) for k in (8, 10, 12, 14)], [(float(f(NF4[6])), 0.0)] + [line(k, -1.0) for k in (4, 2, 0)]


def build(nc, x, gate_codes, gate_scales, up_codes, up_scales, down_codes, down_scales, out):
    NB, C, H = x.shape
    I = gate_codes.shape[0]
    QB = 64
    NQ = C // P
    CH = NB * P
    KT = H // P
    FT = I // P
    REST = I - FT * P
    NT = FT + 1
    HALF = H // 2
    GB = H // QB
    DB = I // QB
    NU = 3 * FT + 2
    assert REST == QB and NB == 4 and KT == 8 and NQ == 8 and FT % 2 == 1

    XS, WS = 10, 8
    IS = 7

    pos_lines, neg_lines = nf4_lines()

    inter_scr = nc.dram_tensor("inter_scr", [NQ, NB, P, 2, NT * P], F16, kind="Internal").ap()
    wd_scr = nc.dram_tensor("wd_scr", [2, P, NT, 2, HALF], F16, kind="Internal").ap()
    prob_scr_t = nc.dram_tensor("prob_scr", [17, H], F32, kind="Internal")
    prob_scr = prob_scr_t.ap()

    with ExitStack() as ctx:
        def sb(name, shape, dt):
            return ctx.enter_context(nc.sbuf_tensor(name, shape, dt))

        def sem(name):
            return ctx.enter_context(nc.semaphore(name))

        big = sb("big", [P, NQ * 2 * KT * CH], F16)
        XT = big[:, :].rearrange("p (q s k t) -> p q s k t", q=NQ, s=2, k=KT)
        ARENA_KB = 68
        arena = sb("arena", [P, ARENA_KB * 256], F32)

        def carve(kb, size_kb, dt=F32):
            v = arena[:, int(kb * 256):int((kb + size_kb) * 256)]
            return v if dt == F32 else v.bitcast(dt)

        codes = carve(0, 4, I32)
        u_sb = carve(4, 4)
        acc_p = carve(8, 4)
        acc_n = carve(12, 4)
        ring = [carve(16, 4), carve(20, 4)]
        w_f = carve(24, 4)
        w_hl = carve(28, 4, F16).rearrange("p (s j) -> p s j", s=2)
        w_t = carve(32, 16, F16).rearrange("p (b g s k m) -> p b g s k m", b=2, g=2, s=2, k=KT)
        wd_stage = carve(48, 4, F16).rearrange("p (s j) -> p s j", s=2)
        xf = carve(52, 4)
        sil = [carve(56, 2), carve(58, 2)]
        inter_f = [carve(60, 2), carve(62, 2)]
        inter_hl = [carve(64, 2, F16).rearrange("p (s t) -> p s t", s=2),
                    carve(66, 2, F16).rearrange("p (s t) -> p s t", s=2)]
        x_ring = [carve(48, 4), carve(56, 4), carve(60, 4), carve(64, 4)]
        prob_t = xf[0:17, :]

        wd_sb = big[:, 0:2 * NT * 2 * HALF].rearrange("p (e k s h) -> p e k s h", e=2, k=NT, s=2)
        pb0 = 2 * NT * 2 * HALF
        prob_b = big[:, pb0:pb0 + 2 * 16 * HALF].bitcast(F32).rearrange("p (j h) -> p j h", j=16)
        it_sb = [carve(0, 11, F16).rearrange("p (s k t) -> p s k t", s=2, k=NT),
                 carve(11, 11, F16).rearrange("p (s k t) -> p s k t", s=2, k=NT)]
        x2_at = pb0 + 2 * 16 * HALF
        x2 = [big[:, x2_at:x2_at + 2 * NB * HALF].bitcast(F32).rearrange("p (n h) -> p n h", n=NB),
              carve(32, 8).rearrange("p (n h) -> p n h", n=NB)]
        xn2 = carve(22, 8).rearrange("p (n h) -> p n h", n=NB)
        prod = carve(30, 2)
        msg = carve(40, 2)
        ffn = carve(42, 2)
        gate2 = carve(44, 2)
        sg = [carve(46, 2), carve(52, 2)]
        e_b = carve(48, 4)
        o_sb = [carve(56, 2), carve(58, 2)]

        s_g = sb("s_g", [P, NT, GB], F32)
        s_u = sb("s_u", [P, FT, GB], F32)
        s_d = sb("s_d", [P, KT, DB], F32)
        mx = sb("mx", [P, 2 * NT + KT], F32)
        inv = sb("inv", [P, 2 * NT + KT], F32)
        gu_prod = sb("gu_prod", [P, NT], F32)
        f_part = sb("f_part", [P, 1], F32)
        f_all = sb("f_all", [P, 1], F32)
        f_inv = sb("f_inv", [P, 1], F32)
        gate_back = sb("gate_back", [P, NT], F32)
        up_back = sb("up_back", [P, NT], F32)
        st = sb("st", [P, 2, 12], F32)
        mvt = sb("mvt", [P, 2, 2], F32)
        mean = sb("mean", [P, NQ * NB], F32)
        rstd = sb("rstd", [P, NQ * NB], F32)
        y = sb("y", [P, 10], F32)
        eps_t = sb("eps_t", [P, 1], F32)
        junk_v = sb("junk_v", [P, 2 * P], BF16)
        junk_a = sb("junk_a", [P, 2 * P], BF16)
        part = sb("part", [P, 10, 4], F32)
        pair = sb("pair", [P, KT, 10], F32)
        sc = sb("sc", [P, KT, 17], F32)
        mxs = sb("mxs", [P, KT, 4], F32)
        zero = sb("zero", [P, 1], F32)
        fence = sb("fence", [P, 2], F32)
        gb_cur = sb("gb_cur", [P, 2], F32)
        id32 = sb("id32", [P, P], F32)
        id16 = sb("id16", [P, P], F16)

        ps = ctx.enter_context(nc.psum_tensor("ps", [P, 8, 512], F32))
        tp = [ps[:, 4, :].bitcast(F16), ps[:, 5, :].bitcast(F16)]
        xp = [ps[:, 0:2, :].rearrange("p b (k t) -> p (b k) t", t=P),
              ps[:, 2:4, :].rearrange("p b (k t) -> p (b k) t", t=P)]

        scales_in = sem("scales_in")
        idents = sem("idents")
        consts = sem("consts")
        prep = sem("prep")
        f_red = sem("f_red")
        code_in = sem("code_in")
        u_made = sem("u_made")
        lines = sem("lines")
        max_done = sem("max_done")
        v_made = sem("v_made")
        w_made = sem("w_made")
        hilo_made = sem("hilo_made")
        tp_done = sem("tp_done")
        tp_evac = sem("tp_evac")
        wd_out = sem("wd_out")
        x_in = [sem(f"x_in{r}") for r in range(4)]
        bn_done = sem("bn_done")
        mv_done = sem("mv_done")
        root = sem("root")
        newton = sem("newton")
        rstd_made = sem("rstd_made")
        xn_ready = sem("xn_ready")
        xt_done = sem("xt_done")
        x_hi = sem("x_hi")
        x_lo = sem("x_lo")
        g_done = sem("g_done")
        up_done = sem("up_done")
        silu_done = sem("silu_done")
        inter_made = sem("inter_made")
        ihl_made = sem("ihl_made")
        inter_out = [sem("inter_out0"), sem("inter_out1")]
        xf_made = sem("xf_made")
        ttr_done = sem("ttr_done")
        sq_done = sem("sq_done")
        pair_made = sem("pair_made")
        gb_made = sem("gb_made")
        fenced = sem("fenced")
        soft = sem("soft")
        soft2 = sem("soft2")
        expd = sem("expd")
        pt_done = sem("pt_done")
        pt_evac = sem("pt_evac")
        prob_out = sem("prob_out")
        wd_in = [sem("wd_in0"), sem("wd_in1")]
        pb_in = sem("pb_in")
        e_in = sem("e_in")
        it_in = [sem("it_in0"), sem("it_in1")]
        x2_in = [sem("x2_in0"), sem("x2_in1")]
        xn2_made = sem("xn2_made")
        y_done = sem("y_done")
        msg_step = sem("msg_step")
        ffn_made = sem("ffn_made")
        g2_made = sem("g2_made")
        sg_made = sem("sg_made")
        o_made = sem("o_made")
        o_out = [sem("o_out0"), sem("o_out1")]

        def unit(i, a):
            return 2 + 3 * i + a

        def kind_of(i, a):
            if isinstance(i, int) and i == FT - 1:
                return [("last", FT), ("down", FT - 1), ("down_last", FT)][a]
            return [("gate", i + 1), ("up", i + 1), ("down", i)][a]

        def attend_chunk(att, par, q):
            return None if att is None or q < 6 else 2 * par + q - 6

        def phase1(eng, tile, done_first=None):
            tile(0, 0, None)
            tile(1, 1, None)
            with eng.Fori(1, KT + 1) as pr:
                tile(pr * 2, 0, pr - 1)
                tile(pr * 2 + 1, 1, pr - 1)
            for i in range(2 * KT + 2, FT + 1):
                tile(i, i % 2, None)

        def is_first(i):
            return isinstance(i, int) and i < 2

        block = ctx.enter_context(nc.Block())

        @block.sync
        def _(sp):
            sp.dma_start(s_g[:, 0:FT, :], gate_scales[0:FT * P, :].rearrange("(i p) b -> p i b", p=P)).then_inc(scales_in, 16)
            sp.dma_start(s_g[0:REST, FT, :], gate_scales[FT * P:I, :]).then_inc(scales_in, 16)
            sp.dma_start(s_g[REST:P, FT, :], up_scales[FT * P:I, :]).then_inc(scales_in, 16)
            sp.dma_start(s_u[:, :, :], up_scales[0:FT * P, :].rearrange("(i p) b -> p i b", p=P)).then_inc(scales_in, 16)
            sp.dma_start(s_d[:, :, :], down_scales.rearrange("(t p) b -> p t b", p=P)).then_inc(scales_in, 16)

            def load_codes(w, kind, t):
                if not (isinstance(w, int) and w == 0):
                    sp.wait_ge(u_made, w)
                if kind in ("gate", "up"):
                    src = gate_codes if kind == "gate" else up_codes
                    for a in (0, 64):
                        sp.dma_start(codes[a:a + 64, :], src[bass.ds(t * P + a, 64), :]).then_inc(code_in, 16)
                elif kind == "last":
                    sp.dma_start(codes[0:REST, :], gate_codes[FT * P:I, :]).then_inc(code_in, 16)
                    sp.dma_start(codes[REST:P, :], up_codes[FT * P:I, :]).then_inc(code_in, 16)
                else:
                    n = P if kind == "down" else REST
                    dst = codes[:, 0:KT * n].rearrange("p (t c) -> p t c", c=n)
                    src = down_codes.rearrange("(t p) i -> p t i", p=P)
                    for a in (4, 0):
                        sp.dma_start(dst[:, a:a + 4, :], src[:, a:a + 4, bass.ds(t * P, n)]).then_inc(code_in, 16)

            def load_x(q, n):
                if not (isinstance(q, int) and q == 0):
                    sp.wait_ge(xt_done, q * 4 + (n - 3))
                sp.dma_start(x_ring[n], x[n, bass.ds(q * P, P), :]).then_inc(x_in[n], 16)

            load_codes(0, "gate", 0)
            for n in range(NB):
                load_x(0, n)
            load_codes(1, "up", 0)
            load_codes(2, "gate", 1)
            with sp.Fori(1, NQ) as q:
                for n in range(NB):
                    load_x(q, n)

            def store_wd(i, t, kind):
                w = unit(i, 2) if kind == "down" and not (isinstance(i, int) and i == FT - 1) else unit(i, t - FT + 2)
                rows = P if kind == "down" else REST
                sp.wait_ge(tp_evac, w * 2 + 2)
                for hh in (0, 1):
                    sp.dma_start(wd_scr[hh, 0:rows, bass.ds(t, 1), :, :].rearrange("p o s h -> p (o s) h"),
                                 wd_stage[0:rows, :, hh * HALF:(hh + 1) * HALF]).then_inc(wd_out, 16)

            def tile(i, par, att):
                last = isinstance(i, int) and i == FT
                for q in range(NQ):
                    if not last and q == 1:
                        load_codes(unit(i, 1), *kind_of(i, 1))
                    if not last and q == 3:
                        load_codes(unit(i, 2), *kind_of(i, 2))
                    if not (isinstance(i, int) and i >= FT - 1) and q == 5:
                        nxt = i + 1
                        load_codes(unit(nxt, 0), *kind_of(nxt, 0))
                    if isinstance(i, int) and i == FT - 1 and q == 5:
                        store_wd(i, FT - 1, "down")
                    if not last and q == 7:
                        k, t = kind_of(i, 2)
                        store_wd(i, t, k)
                    sp.wait_ge(ihl_made, (i * NQ + q) * 2 + 2)
                    rows = slice(REST, P) if last else slice(0, P)
                    n_rows = REST if last else P
                    for s in (1, 0):
                        sp.dma_start(
                            inter_scr[q, :, 0:n_rows, s, bass.ds(i * P, P)].rearrange("n p t -> p n t"),
                            inter_hl[q % 2][rows, s, :].rearrange("p (n t) -> p n t", n=NB),
                        ).then_inc(inter_out[q % 2], 16)
                    if isinstance(i, int) and i == FT - 2 and q == 7:
                        sp.wait_ge(pt_evac, 1)
                        sp.dma_start(prob_scr[:, :], prob_t).then_inc(prob_out, 16)
                    if last:
                        load_wd(q)

            per = XT.shape[2] * XT.shape[3] * CH // (2 * HALF)
            pieces = {0: [(0, 0, 8)], 1: [(0, 8, 16)], 2: [(0, 16, NT)], 3: [(1, 0, 10)], 5: [(1, 10, NT)]}

            def load_wd(q):
                for e, a, b in pieces.get(q, []):
                    assert (e * NT + b - 1) // per <= q
                    if q == 0:
                        sp.wait_ge(wd_out, 32 * NT)
                    sp.wait_ge(g_done, FT * NQ + q + 1)
                    full = min(b, FT)
                    sp.dma_start(wd_sb[:, e, a:full, :, :].rearrange("p k s h -> p (k s h)"),
                                 wd_scr[e, :, a:full, :, :].rearrange("p k s h -> p (k s h)")).then_inc(wd_in[e], 16)
                    if b == NT:
                        sp.dma_start(wd_sb[0:REST, e, FT, :, :], wd_scr[e, 0:REST, FT, :, :]).then_inc(wd_in[e], 16)

            phase1(sp, tile)

            sp.wait_ge(inter_out[0], 32 * NT * NQ // 2)
            sp.wait_ge(inter_out[1], 32 * NT * NQ // 2)
            sp.wait_ge(prob_out, 16)

            def load_inter(e, q, n):
                s = (e * NQ + q) * NB + n
                if not (isinstance(q, int) and s < 2):
                    sp.wait_ge(y_done, s - 1)
                dst = it_sb[n % 2]
                src = inter_scr[bass.ds(q, 1), n, :, :, :].rearrange("o p s c -> (o p) s c")
                sp.dma_start(dst[:, :, 0:FT, :].rearrange("p s k t -> p s (k t)"), src[:, :, 0:FT * P]).then_inc(it_in[n % 2], 16)
                sp.dma_start(dst[0:REST, :, FT, :], src[0:REST, :, FT * P:NT * P]).then_inc(it_in[n % 2], 16)

            def load_x2(e, q, b):
                if not (isinstance(q, int) and e == 0 and q < 2):
                    sp.wait_ge(o_made, (e * NQ + q - 1) * NB)
                sp.dma_start(x2[b], x[:, bass.ds(q * P, P), e * HALF:(e + 1) * HALF].rearrange("n p h -> p n h")).then_inc(x2_in[b], 16)

            def load_prob(e):
                src = bass.AP(prob_scr_t, e * HALF, [[0, P], [H, 16], [1, HALF]])
                sp.dma_start(prob_b, src).then_inc(pb_in, 16)

            def store_out(e, q, n):
                s = (e * NQ + q) * NB + n
                sp.wait_ge(o_made, s + 1)
                sp.dma_start(out[n, bass.ds(q * P, P), e * HALF:(e + 1) * HALF], o_sb[n % 2]).then_inc(o_out[n % 2], 16)

            load_inter(0, 0, 0)
            load_inter(0, 0, 1)
            load_x2(0, 0, 0)
            load_prob(0)
            sp.dma_start(e_b, bass.AP(prob_scr_t, 16 * H, [[0, P], [1, H]])).then_inc(e_in, 16)

            def half(e, q, b, final=False):
                for n in range(NB):
                    if n == 0 and not final:
                        load_x2(e, q + 1, 1 - b)
                    if n < 2:
                        load_inter(e, q, n + 2)
                    elif not final:
                        load_inter(e, q + 1, n - 2)
                    store_out(e, q, n)

            for e in (0, 1):
                if e == 1:
                    load_inter(1, 0, 0)
                    load_inter(1, 0, 1)
                    load_x2(1, 0, 0)
                    sp.wait_ge(msg_step, 7 * NQ * NB)
                    load_prob(1)
                half(e, 0, 0)
                half(e, 1, 1)
                with sp.Fori(1, NQ // 2 - 1) as pr:
                    half(e, pr * 2, 0)
                    half(e, pr * 2 + 1, 1)
                half(e, NQ - 2, 0)
                half(e, NQ - 1, 1, final=True)
            for b in (0, 1):
                sp.wait_ge(o_out[b], 16 * NQ * NB)

        @block.gpsimd
        def _(pool):
            g = nc.gpsimd
            g.memset(id32[:], 0.0).then_inc(idents, 1)
            g.memset(zero[:, :], 0.0).then_inc(idents, 1)
            pool.wait_ge(idents, 2)
            g.affine_select(out=id32[:], in_=id32[:], compare_op=ALU.not_equal, fill=1.0, base=0,
                            pattern=[[-1, P]], channel_multiplier=1).then_inc(idents, 1)
            pool.wait_ge(idents, 3)
            g.tensor_copy(id16[:], id32[:]).then_inc(idents, 1)

            def hilo(w, n=1024):
                pool.wait_ge(w_made, w + 1)
                if not (isinstance(w, int) and w == 0):
                    pool.wait_ge(tp_done, w)
                g.tensor_tensor(w_hl[:, 0, 0:n], w_f[:, 0:n], zero[:, 0:1].to_broadcast([P, n]), ALU.add).then_inc(hilo_made, 1)
                pool.wait_ge(hilo_made, w * 2 + 1)
                g.tensor_tensor(w_hl[:, 1, 0:n], w_f[:, 0:n], w_hl[:, 0, 0:n], ALU.subtract).then_inc(hilo_made, 1)

            pool.wait_ge(prep, 10)
            g.partition_all_reduce(f_all[:, :], f_part[:, :], P, RMAX).then_inc(f_red, 1)
            hilo(0)
            hilo(1)

            def size(i, a):
                return KT * REST if kind_of(i, a)[0] == "down_last" else 1024

            def tile(i, par, att):
                last = isinstance(i, int) and i == FT
                rows = slice(REST, P) if last else slice(0, P)
                for q in range(NQ):
                    if not last and q in (1, 3, 5):
                        a = q // 2
                        hilo(unit(i, a), size(i, a))
                    j = attend_chunk(att, par, q)
                    if j is not None:
                        c = att * 4 + j
                        if j == 0:
                            pool.wait_ge(pair_made, att + 1)
                        else:
                            pool.wait_ge(ttr_done, c * 6)
                            pool.wait_ge(sq_done, c * 4)
                        v = [XT[:, 2 * j:2 * j + 2, s, bass.ds(att, 1), :].rearrange("p q o t -> p q (o t)") for s in (0, 1)]
                        g.tensor_tensor(xf.rearrange("p (q t) -> p q t", q=2), v[0], v[1], ALU.add).then_inc(xf_made, 1)
                    k = i * NQ + q
                    if last and q == 0:
                        pool.wait_ge(ihl_made, k * 2)
                    pool.wait_ge(inter_made, k + 1)
                    if not (isinstance(k, int) and k < 2):
                        pool.wait_ge(inter_out[q % 2], (i * 4 + q // 2) * 32)
                    hi, lo = inter_hl[q % 2][rows, 0, :], inter_hl[q % 2][rows, 1, :]
                    src = inter_f[q % 2][rows, :]
                    g.tensor_tensor(hi, src, zero[rows, 0:1].to_broadcast([rows.stop - rows.start, CH]), ALU.add).then_inc(ihl_made, 1)
                    pool.wait_ge(ihl_made, k * 2 + 1)
                    g.tensor_tensor(lo, src, hi, ALU.subtract).then_inc(ihl_made, 1)

            phase1(pool, tile)
            pool.wait_ge(ihl_made, NT * NQ * 2)

            def half(e, q, b):
                for n in range(NB):
                    s = (e * NQ + q) * NB + n
                    pool.wait_ge(sg_made, s + 1)
                    if not (isinstance(s, int) and s < 2):
                        pool.wait_ge(o_out[n % 2], (e * NQ + q) * 32 + (n // 2) * 16)
                    g.tensor_tensor(o_sb[n % 2], sg[n % 2], x2[b][:, n, :], ALU.add).then_inc(o_made, 1)

            for e in (0, 1):
                half(e, 0, 0)
                half(e, 1, 1)
                with pool.Fori(1, NQ // 2) as pr:
                    half(e, pr * 2, 0)
                    half(e, pr * 2 + 1, 1)

        @block.scalar
        def _(act):
            a_ = nc.scalar

            def line_set(w, second, n=1024):
                first = isinstance(w, int) and w == 0
                for j, (slope, offset) in enumerate(neg_lines if second else pos_lines):
                    c = (3 if second else 0) + j - 1
                    if j == 0:
                        if not second:
                            act.wait_ge(u_made, w + 1)
                            if not first:
                                act.wait_ge(w_made, w)
                        dst = acc_n if second else acc_p
                    else:
                        if c >= 2:
                            act.wait_ge(max_done, w * 6 + c - 1)
                        dst = ring[c % 2]
                    if second and j == 0:
                        a_.activation(dst[:, 0:n], u_sb[:, 0:n], ACT.Relu, scale=slope).then_inc(lines, 1)
                    else:
                        a_.activation(dst[:, 0:n], u_sb[:, 0:n], ACT.Copy, bias=offset, scale=slope).then_inc(lines, 1)

            for w in (0, 1):
                line_set(w, False)
                line_set(w, True)

            act.wait_ge(consts, 1)

            def x_batch(q, h, first=False, final=False):
                b = q * 2 + h
                if not final:
                    act.wait_ge(mv_done, b * 2 + 2)
                    if not first:
                        act.wait_ge(newton, b * 5)
                    vin = mvt[:, :, 1]
                    a_.activation(y[:, 0:2], vin, ACT.Sqrt, bias=eps_t[:, 0:1], scale=2.0 ** (-2 * XS)).then_inc(root, 1)
                if not first:
                    pq, ph = (q, 0) if h else (q - 1, 1)
                    for j in (0, 1):
                        n = 2 * ph + j
                        if not (isinstance(pq, int) and pq * 4 + n == 0):
                            act.wait_ge(fenced, pq * 4 + n)
                        act.wait_ge(xt_done, pq * 4 + n + 1)
                        a_.activation(fence[:, 0:1], eps_t[:, 0:1], ACT.Copy).then_inc(fenced, 1)
                        dst = XT[:, bass.ds(pq, 1), 0, :, n * P:(n + 1) * P].rearrange("p o k t -> p (o k) t")
                        a_.activation(dst, xp[n % 2], ACT.Copy).then_inc(x_hi, 1)

            x_batch(0, 0, first=True)
            x_batch(0, 1)
            with act.Fori(1, NQ) as q:
                x_batch(q, 0)
                x_batch(q, 1)
            x_batch(NQ, 0, final=True)

            def tile(i, par, att):
                last = isinstance(i, int) and i == FT
                for q in range(NQ):
                    if not last and q < 6:
                        a = q // 2
                        n = KT * REST if kind_of(i, a)[0] == "down_last" else 1024
                        line_set(unit(i, a), q % 2 == 1, n)
                    j = attend_chunk(att, par, q)
                    if j is not None:
                        act.wait_ge(xf_made, att * 4 + j + 1)
                        if j == 0:
                            act.wait_ge(pair_made, att + 1)
                        v = xf.rearrange("p (q n t) -> p q n t", q=2, n=NB)
                        for n in range(NB):
                            at = [0, 4, 7, 9][n]
                            if n:
                                act.wait_ge(sq_done, (att * 4 + j) * 4 + n)
                            a_.activation(junk_a[:, :].rearrange("p (q t) -> p q t", q=2), v[:, :, n, :], ACT.Square,
                                                accum_out=part[:, at, j:j + 1]).then_inc(sq_done, 1)
                    if isinstance(i, int) and i == FT - 3 and q == 6:
                        act.wait_ge(soft2, 2 * NB)
                        a_.activation(sc[:, :, 0:16], sc[:, :, 0:16], ACT.Exp, scale=2.0 ** (-2 * XS) / float(H) ** 0.5).then_inc(expd, 1)
                    k = i * NQ + q
                    act.wait_ge(g_done, k + 1)
                    if not (isinstance(k, int) and k < 2):
                        act.wait_ge(inter_made, k - 1)
                    src = ps[0:REST, q % 2, :] if last else ps[:, q % 2, :]
                    dst = sil[q % 2][REST:P, :] if last else sil[q % 2]
                    scale = gb_cur[0:REST, par:par + 1] if last else gb_cur[:, par:par + 1]
                    if q == 0:
                        act.wait_ge(gb_made, i + 1)
                    a_.activation(dst, src, ACT.Silu, scale=scale).then_inc(silu_done, 1)

            phase1(act, tile)

            def half(e, q, b):
                for n in range(NB):
                    s = (e * NQ + q) * NB + n
                    act.wait_ge(ffn_made, s + 1)
                    if not (isinstance(s, int) and s < 1):
                        act.wait_ge(sg_made, s)
                    a_.activation(gate2, ffn, ACT.Silu).then_inc(g2_made, 1)

            for e in (0, 1):
                half(e, 0, 0)
                half(e, 1, 1)
                with act.Fori(1, NQ // 2) as pr:
                    half(e, pr * 2, 0)
                    half(e, pr * 2 + 1, 1)

        @block.vector
        def _(dve):
            v_ = nc.vector
            v_.memset(part[:, :, :], 0.0).then_inc(pair_made, 1)
            v_.memset(eps_t[:, :], EPS * 2.0 ** (-2 * XS)).then_inc(consts, 1)

            steps = [0]

            def step(ins, wait=True):
                ins.then_inc(prep, 1)
                steps[0] += 1
                if wait:
                    dve.wait_ge(prep, steps[0])

            dve.wait_ge(scales_in, 16 * 5)
            step(v_.tensor_reduce(mx[:, 0:NT], s_g[:, :, :], AX.X, ALU.max, apply_absolute_value=True), False)
            step(v_.tensor_reduce(mx[:, NT:NT + FT], s_u[:, :, :], AX.X, ALU.max, apply_absolute_value=True), False)
            step(v_.tensor_reduce(mx[:, 2 * NT:], s_d[:, :, :], AX.X, ALU.max, apply_absolute_value=True))
            step(v_.tensor_copy(mx[:, 2 * NT - 1:2 * NT], mx[:, NT - 1:NT]))
            step(v_.tensor_scalar(mx[:, :], mx[:, :], 2.0 ** -60, None, ALU.max))
            mi = mx[:, :].bitcast(I32)
            step(v_.tensor_scalar(mi, mi, 0x7F800000, None, ALU.bitwise_and))
            step(v_.reciprocal(inv[:, :], mx[:, :]))
            step(v_.tensor_scalar(inv[:, :], inv[:, :], 2.0 ** WS, None, ALU.mult))
            step(v_.tensor_tensor(gu_prod[:, :], mx[:, 0:NT], mx[:, NT:2 * NT], ALU.mult))
            step(v_.tensor_reduce(f_part[:, :], gu_prod[:, :], AX.X, ALU.max))
            step(v_.tensor_tensor(s_g[:, :, :], s_g[:, :, :], inv[:, 0:NT].unsqueeze(2).to_broadcast([P, NT, GB]), ALU.mult), False)
            step(v_.tensor_tensor(s_u[:, :, :], s_u[:, :, :], inv[:, NT:NT + FT].unsqueeze(2).to_broadcast([P, FT, GB]), ALU.mult), False)
            step(v_.tensor_tensor(s_d[:, :, :], s_d[:, :, :], inv[:, 2 * NT:].unsqueeze(2).to_broadcast([P, KT, DB]), ALU.mult), False)
            step(v_.tensor_scalar(gate_back[:, :], mx[:, 0:NT], 2.0 ** (-XS - WS), None, ALU.mult))
            dve.wait_ge(f_red, 1)
            step(v_.reciprocal(f_inv[:, :], f_all[:, :]))
            step(v_.tensor_scalar(up_back[:, :], mx[:, NT:2 * NT], f_inv[:, 0:1], 2.0 ** (-XS - WS - IS), ALU.mult, ALU.mult), False)
            step(v_.tensor_scalar(sc[:, :, 16:17].rearrange("p t o -> p (t o)"), mx[:, 2 * NT:], f_all[:, 0:1], 2.0 ** (IS - WS), ALU.mult, ALU.mult))

            def shift(w, n=1024):
                dve.wait_ge(code_in, w * 32 + 32)
                if not (isinstance(w, int) and w == 0):
                    dve.wait_ge(lines, w * 8)
                v_.tensor_scalar(u_sb[:, 0:n], codes[:, 0:n], -7.0, None, ALU.add).then_inc(u_made, 1)

            def maxima(w, second, n=1024):
                acc = acc_n if second else acc_p
                for j in (1, 2, 3):
                    c = (3 if second else 0) + j - 1
                    dve.wait_ge(lines, w * 8 + (4 if second else 0) + j + 1)
                    if j > 1:
                        dve.wait_ge(max_done, w * 6 + c)
                    v_.tensor_tensor(acc[:, 0:n], acc[:, 0:n], ring[c % 2][:, 0:n], ALU.max).then_inc(max_done, 1)

            def dequant(w, kind, t, n=1024):
                dve.wait_ge(max_done, w * 6 + 6)
                v_.scalar_tensor_tensor(acc_p[:, 0:n], acc_p[:, 0:n], 0.0, acc_n[:, 0:n], ALU.max, ALU.subtract).then_inc(v_made, 1)
                dve.wait_ge(v_made, w + 1)
                if not (isinstance(w, int) and w == 0):
                    dve.wait_ge(hilo_made, w * 2)
                if kind in ("gate", "up", "last"):
                    tab = s_u if kind == "up" else s_g
                    s = tab[:, bass.ds(t, 1), :].rearrange("p o b -> p (o b)")
                    shape, split = [P, GB, QB], "p (b c) -> p b c"
                    v_.tensor_tensor(w_f[:, :].rearrange(split, c=QB), acc_p[:, :].rearrange(split, c=QB),
                                     s.unsqueeze(2).to_broadcast(shape), ALU.mult).then_inc(w_made, 1)
                else:
                    nb = n // KT // QB
                    for b in range(nb):
                        s = s_d[:, :, bass.ds(t * 2 + b, 1)]
                        d = w_f[:, 0:n].rearrange("p (t b c) -> p t b c", t=KT, c=QB)[:, :, b, :]
                        a = acc_p[:, 0:n].rearrange("p (t b c) -> p t b c", t=KT, c=QB)[:, :, b, :]
                        ins = v_.tensor_tensor(d, a, s.to_broadcast([P, KT, QB]), ALU.mult)
                    ins.then_inc(w_made, 1)

            def evacuate(w, kind, par, d=None):
                dve.wait_ge(tp_done, w + 1)
                if kind in ("gate", "up", "last"):
                    gu = 1 if kind == "up" else 0
                    for s in (0, 1):
                        v_.tensor_copy(w_t[:, par, gu, s, :, :].rearrange("p k m -> p (k m)"), tp[s]).then_inc(tp_evac, 1)
                else:
                    if not (isinstance(d, int) and d == 0):
                        dve.wait_ge(wd_out, d * 32)
                    rows = P if kind == "down" else REST
                    for s in (0, 1):
                        v_.tensor_copy(wd_stage[0:rows, s, :], tp[s][0:rows, :]).then_inc(tp_evac, 1)

            shift(0)
            for w, kind in ((0, "gate"), (1, "up")):
                maxima(w, False)
                maxima(w, True)
                shift(w + 1)
                dequant(w, kind, 0)
                evacuate(w, kind, 0)

            v_.tensor_scalar(gb_cur[:, 0:1], gate_back[:, 0:1], 1.0, None, ALU.mult).then_inc(gb_made, 1)

            def x_lo_part(q, h):
                for j in (0, 1):
                    n = 2 * h + j
                    dve.wait_ge(x_hi, q * 4 + n + 1)
                    hi, lo = [XT[:, bass.ds(q, 1), s, :, n * P:(n + 1) * P].rearrange("p o k t -> p (o k) t") for s in (0, 1)]
                    v_.tensor_tensor(lo, xp[n % 2], hi, ALU.subtract).then_inc(x_lo, 1)

            def x_batch(q, h, first=False):
                b = q * 2 + h
                for j in (0, 1):
                    n = 2 * h + j
                    dve.wait_ge(x_in[n], q * 16 + 16)
                    for m in (0, 1):
                        v_.bn_stats(st[:, j, 6 * m:6 * m + 6], x_ring[n][:, m * 512:(m + 1) * 512]).then_inc(bn_done, 1)
                dve.wait_ge(bn_done, b * 4 + 4)
                v_.tensor_scalar(fence[:, 1:2], eps_t[:, 0:1], 1.0, None, ALU.mult)
                for j in (0, 1):
                    v_.bn_aggr(mvt[:, j, :], st[:, j, :]).then_inc(mv_done, 1)
                if not first:
                    x_lo_part(*((q, 0) if h else (q - 1, 1)))
                vin = mvt[:, :, 1]
                dve.wait_ge(mv_done, b * 2 + 2)
                v_.tensor_scalar(y[:, 2:4], vin, EPS, 2.0 ** (-2 * XS), ALU.add, ALU.mult).then_inc(newton, 1)
                dve.wait_ge(root, b + 1)
                v_.reciprocal(y[:, 4:6], y[:, 0:2]).then_inc(newton, 1)
                dve.wait_ge(newton, b * 5 + 2)
                v_.tensor_tensor(y[:, 4:6], y[:, 4:6], y[:, 2:4], ALU.mult).then_inc(newton, 1)
                dve.wait_ge(newton, b * 5 + 3)
                v_.tensor_tensor(y[:, 6:8], y[:, 4:6], y[:, 0:2], ALU.add).then_inc(newton, 1)
                dve.wait_ge(newton, b * 5 + 4)
                v_.tensor_scalar(y[:, 6:8], y[:, 6:8], 0.5, None, ALU.mult).then_inc(newton, 1)
                dve.wait_ge(newton, b * 5 + 5)
                v_.reciprocal(y[:, 8:10], y[:, 6:8]).then_inc(rstd_made, 1)
                dve.wait_ge(rstd_made, b + 1)
                v_.tensor_scalar(rstd[:, bass.ds(b * 2, 2)], y[:, 8:10], 1.0, None, ALU.mult)
                v_.tensor_scalar(mean[:, bass.ds(b * 2, 2)], mvt[:, :, 0], 1.0, None, ALU.mult)
                for j in (0, 1):
                    n = 2 * h + j
                    v_.tensor_scalar(x_ring[n], x_ring[n], mvt[:, j, 0:1], y[:, 8 + j:9 + j], ALU.subtract, ALU.mult).then_inc(xn_ready, 1)

            x_batch(0, 0, first=True)
            x_batch(0, 1)
            with dve.Fori(1, NQ) as q:
                x_batch(q, 0)
                x_batch(q, 1)
            x_lo_part(NQ - 1, 1)

            PAIRS = [(n, m) for n in range(NB) for m in range(n, NB)]

            def softmax():
                c = [0]

                def st_(ins):
                    c[0] += 1
                    ins.then_inc(soft, 1)
                    dve.wait_ge(soft, c[0])

                dve.wait_ge(pair_made, KT + 1)
                at = 0
                for n in range(NB):
                    k = NB - n
                    st_(v_.tensor_copy(sc[:, :, 4 * n + n:4 * n + 4], pair[:, :, at:at + k]))
                    if k > 1:
                        st_(v_.tensor_copy(sc[:, :, 4 * (n + 1) + n:4 * (NB - 1) + n + 1:4], pair[:, :, at + 1:at + k]))
                    at += k
                s3 = [sc[:, :, 4 * n:4 * n + 4] for n in range(NB)]
                for n in range(NB):
                    v_.tensor_reduce(mxs[:, :, n:n + 1], s3[n], AX.X, ALU.max).then_inc(soft2, 1)
                dve.wait_ge(soft2, NB)
                for n in range(NB):
                    v_.tensor_tensor(s3[n], s3[n], mxs[:, :, n:n + 1].to_broadcast([P, KT, NB]), ALU.subtract).then_inc(soft2, 1)
                dve.wait_ge(soft2, 2 * NB)

            def softmax_end():
                dve.wait_ge(expd, 1)
                s3 = [sc[:, :, 4 * n:4 * n + 4] for n in range(NB)]
                for n in range(NB):
                    v_.tensor_reduce(mxs[:, :, n:n + 1], s3[n], AX.X, ALU.add).then_inc(soft2, 1)
                dve.wait_ge(soft2, 3 * NB)
                v_.reciprocal(mxs[:, :, :], mxs[:, :, :]).then_inc(soft2, 1)
                dve.wait_ge(soft2, 3 * NB + 1)
                for n in range(NB):
                    v_.tensor_tensor(s3[n], s3[n], mxs[:, :, n:n + 1].to_broadcast([P, KT, NB]), ALU.mult).then_inc(soft2, 1)
                dve.wait_ge(soft2, 4 * NB + 1)
                diag = sc[:, :, 0:16:5]
                v_.tensor_scalar(diag, diag, 1.0, None, ALU.add).then_inc(soft2, 1)
                dve.wait_ge(soft2, 4 * NB + 2)
                v_.tensor_scalar(sc[:, :, 0:16], sc[:, :, 0:16], 2.0 ** -XS, None, ALU.mult).then_inc(soft2, 1)

            def tile(i, par, att):
                last = isinstance(i, int) and i == FT
                rows = slice(REST, P) if last else slice(0, P)
                for q in range(NQ):
                    if not last and q < 6:
                        a = q // 2
                        kind, t = kind_of(i, a)
                        n = KT * REST if kind == "down_last" else 1024
                        maxima(unit(i, a), q % 2 == 1, n)
                        if q % 2:
                            if a < 2:
                                shift(unit(i, a + 1), KT * REST if kind_of(i, a + 1)[0] == "down_last" else 1024)
                            elif not (isinstance(i, int) and i == FT - 1):
                                shift(unit(i, 3))
                            dequant(unit(i, a), kind, t, n)
                    j = attend_chunk(att, par, q)
                    if j is not None:
                        dve.wait_ge(xf_made, att * 4 + j + 1)
                        xv = xf.rearrange("p (q n t) -> p q n t", q=2, n=NB)
                        done = 0
                        for at, (n, m) in enumerate(PAIRS):
                            if n != m:
                                if done:
                                    dve.wait_ge(ttr_done, (att * 4 + j) * 6 + done)
                                done += 1
                                v_.tensor_tensor_reduce(
                                    junk_v[:, :].rearrange("p (q t) -> p q t", q=2), xv[:, :, n, :], xv[:, :, m, :], 1.0, 0.0,
                                    ALU.mult, ALU.add, part[:, at, j:j + 1]).then_inc(ttr_done, 1)
                        if j == 3:
                            dve.wait_ge(ttr_done, att * 24 + 24)
                            dve.wait_ge(sq_done, att * 16 + 16)
                            v_.tensor_reduce(pair[:, bass.ds(att, 1), :].rearrange("p o c -> p (o c)"), part[:, :, :], AX.X, ALU.add).then_inc(pair_made, 1)
                    if isinstance(i, int) and i == FT - 3:
                        if q == 6:
                            softmax()
                        if q == 7:
                            softmax_end()
                    if isinstance(i, int) and i == FT - 2 and q == 6:
                        dve.wait_ge(pt_done, 1)
                        v_.tensor_copy(prob_t, ps[0:17, 6:8, :].rearrange("p b c -> p (b c)")).then_inc(pt_evac, 1)
                    if not last and q == 7:
                        v_.tensor_scalar(gb_cur[:, 1 - par:2 - par], gate_back[:, bass.ds(i + 1, 1)], 1.0, None, ALU.mult).then_inc(gb_made, 1)
                    if not last and q in (3, 5, 7):
                        a = q // 2 - 1
                        kind, t = kind_of(i, a)
                        d = None if kind not in ("down", "down_last") else t
                        evacuate(unit(i, a), kind, 1 - par, d)
                    k = i * NQ + q
                    dve.wait_ge(silu_done, k + 1)
                    if last:
                        dve.wait_ge(g_done, k + 1)
                    else:
                        dve.wait_ge(up_done, k + 1)
                    if not (isinstance(k, int) and k < 2):
                        dve.wait_ge(ihl_made, (k - 1) * 2)
                    src = ps[rows, q % 2, :] if last else ps[:, 2 + q % 2, :]
                    v_.scalar_tensor_tensor(inter_f[q % 2][rows, :], src, up_back[rows, bass.ds(i, 1)],
                                            sil[q % 2][rows, :], ALU.mult, ALU.mult).then_inc(inter_made, 1)

            phase1(dve, tile)

            dve.wait_ge(e_in, 16)

            def half(e, q, b):
                qq = e * NQ + q
                dve.wait_ge(x2_in[b], (qq // 2 if isinstance(qq, int) else pr_uses(e, q)) * 16 + 16)
                if not (isinstance(qq, int) and qq == 0):
                    dve.wait_ge(msg_step, qq * NB * 7)
                for m in range(NB):
                    v_.tensor_scalar(xn2[:, m, :], x2[b][:, m, :], mean[:, bass.ds(q * 4 + m, 1)],
                                     rstd[:, bass.ds(q * 4 + m, 1)], ALU.subtract, ALU.mult).then_inc(xn2_made, 1)
                for n in range(NB):
                    s = qq * NB + n
                    base = s * 7
                    if not (isinstance(s, int) and s == 0):
                        dve.wait_ge(sg_made, s)
                    for m in range(NB):
                        dve.wait_ge(xn2_made, qq * NB + m + 1)
                        if m >= 2:
                            dve.wait_ge(msg_step, base + 2 * m - 1)
                        v_.tensor_tensor(msg if m == 0 else prod, prob_b[:, 4 * n + m, :], xn2[:, m, :], ALU.mult).then_inc(msg_step, 1)
                        if m > 0:
                            dve.wait_ge(msg_step, base + 2 * m)
                            v_.tensor_tensor(msg, msg, prod, ALU.add).then_inc(msg_step, 1)
                    dve.wait_ge(y_done, s + 1)
                    if not (isinstance(s, int) and s == 0):
                        dve.wait_ge(g2_made, s)
                    v_.tensor_tensor(ffn, ps[:, n, :], e_b[:, e * HALF:(e + 1) * HALF], ALU.mult).then_inc(ffn_made, 1)
                    dve.wait_ge(g2_made, s + 1)
                    dve.wait_ge(msg_step, base + 7)
                    if not (isinstance(s, int) and s < 2):
                        dve.wait_ge(o_made, s - 1)
                    v_.tensor_tensor(sg[n % 2], msg, gate2, ALU.mult).then_inc(sg_made, 1)

            def pr_uses(e, q):
                raise AssertionError

            for e in (0, 1):
                dve.wait_ge(pb_in, 16 * (e + 1))
                half(e, 0, 0)
                half(e, 1, 1)
                with dve.Fori(1, NQ // 2) as pr:
                    pr_uses = lambda e, q, pr=pr: pr + e * (NQ // 2)
                    half(e, pr * 2, 0)
                    half(e, pr * 2 + 1, 1)

        @block.tensor
        def _(pe):
            t_ = nc.tensor
            pe.wait_ge(idents, 4)

            def transpose_unit(w, kind):
                pe.wait_ge(hilo_made, w * 2 + 2)
                if not (isinstance(w, int) and w == 0):
                    pe.wait_ge(tp_evac, w * 2)
                n = REST if kind == "down_last" else P
                for s in (0, 1):
                    for k in range(KT):
                        ins = t_.transpose(tp[s][0:n, k * P:(k + 1) * P], w_hl[:, s, k * n:(k + 1) * n], id16[:, :])
                ins.then_inc(tp_done, 1)

            transpose_unit(0, "gate")
            transpose_unit(1, "up")

            def transpose_x(q, n):
                pe.wait_ge(xn_ready, q * 4 + n + 1)
                if not (isinstance(q, int) and q * 4 + n < 2):
                    pe.wait_ge(x_lo, q * 4 + n - 1)
                for k in range(KT):
                    ins = t_.transpose(xp[n % 2][:, k, :], x_ring[n][:, k * P:(k + 1) * P], id32[:, :])
                ins.then_inc(xt_done, 1)

            for n in range(NB):
                transpose_x(0, n)
            with pe.Fori(1, NQ) as q:
                for n in range(NB):
                    transpose_x(q, n)

            TERMS = [(0, 0), (0, 1), (1, 0)]

            def tile(i, par, att):
                last = isinstance(i, int) and i == FT
                for q in range(NQ):
                    k_ = i * NQ + q
                    if q == 0:
                        if isinstance(i, int) and i == 0:
                            pe.wait_ge(tp_evac, 4)
                            pe.wait_ge(x_hi, NQ * NB)
                            pe.wait_ge(x_lo, NQ * NB)
                        else:
                            pe.wait_ge(tp_evac, 2 * unit(FT - 1, 0) + 2 if last else i * 6 + 2)
                    if not (isinstance(k_, int) and k_ < 2):
                        pe.wait_ge(silu_done, k_ - 1)
                        if last:
                            pe.wait_ge(inter_made, k_ - 1)
                    for k in range(KT):
                        for a, b in TERMS:
                            ins = t_.matmul(ps[:, q % 2, :], w_t[:, par, 0, a, k, :], XT[:, q, b, k, :],
                                            start=(k == 0 and (a, b) == TERMS[0]), stop=(k == KT - 1 and (a, b) == TERMS[-1]))
                    ins.then_inc(g_done, 1)
                    if not last:
                        if not (isinstance(k_, int) and k_ < 2):
                            pe.wait_ge(inter_made, k_ - 1)
                        for k in range(KT):
                            for a, b in TERMS:
                                ins = t_.matmul(ps[:, 2 + q % 2, :], w_t[:, par, 1, a, k, :], XT[:, q, b, k, :],
                                                start=(k == 0 and (a, b) == TERMS[0]), stop=(k == KT - 1 and (a, b) == TERMS[-1]))
                        ins.then_inc(up_done, 1)
                        if q in (2, 4, 6):
                            a = q // 2 - 1
                            transpose_unit(unit(i, a), kind_of(i, a)[0])
                    if isinstance(i, int) and i == FT - 2 and q == 3:
                        pe.wait_ge(soft2, 4 * NB + 3)
                        for t in range(KT):
                            ins = t_.transpose(ps[0:17, 6 + t // 4, (t % 4) * P:(t % 4 + 1) * P], sc[:, t, :], id32[:, :])
                        ins.then_inc(pt_done, 1)

            phase1(pe, tile)

            pe.wait_ge(silu_done, NT * NQ)
            pe.wait_ge(inter_made, NT * NQ)

            def half(e, q, uses):
                for n in range(NB):
                    s = (e * NQ + q) * NB + n
                    pe.wait_ge(it_in[n % 2], (uses + n // 2) * 32 + 32)
                    if not (isinstance(s, int) and s < NB):
                        pe.wait_ge(ffn_made, s - NB + 1)
                    for k in range(NT):
                        r = P if k < FT else REST
                        for a, b in TERMS:
                            ins = t_.matmul(ps[:, n, :], it_sb[n % 2][0:r, a, k, :], wd_sb[0:r, e, k, b, :],
                                            start=(k == 0 and (a, b) == TERMS[0]), stop=(k == NT - 1 and (a, b) == TERMS[-1]))
                    ins.then_inc(y_done, 1)

            for e, n_in in ((0, 4 * 16), (1, 3 * 16)):
                pe.wait_ge(wd_in[e], n_in)
                half(e, 0, e * NQ * 2)
                with pe.Fori(1, NQ) as q:
                    half(e, q, q * 2 + e * NQ * 2)


_INS = ['L0_attn_x', 'L0_ffn_gate_codes', 'L0_ffn_gate_scales', 'L0_ffn_up_codes', 'L0_ffn_up_scales',
        'L0_ffn_down_codes', 'L0_ffn_down_scales']


def kernel(**inputs):
    import numpy as _np
    import concourse.bacc as _bacc
    from concourse import mybir as _mybir
    from concourse.bass_utils import run_bass_kernel_spmd as _run

    nc = _bacc.Bacc("TRN2", target_bir_lowering=False, num_devices=1)
    arrays, args = {}, []
    for name in _INS:
        a = _np.ascontiguousarray(inputs[name])
        arrays[f"in_{name}"] = a
        args.append(nc.dram_tensor(f"in_{name}", a.shape, _mybir.dt.from_np(a.dtype), kind="ExternalInput").ap())
    shape = arrays["in_L0_attn_x"].shape
    out = nc.dram_tensor("out_0", shape, _mybir.dt.float32, kind="ExternalOutput").ap()
    build(nc, *args, out)
    r = _run(nc, [arrays], core_ids=[0])
    return r.results[0]["out_0"]
```

```python
from contextlib import ExitStack

import numpy as np
import concourse.bass as bass
from concourse import mybir

ALU = mybir.AluOpType
ACT = mybir.ActivationFunctionType
AX = mybir.AxisListType
F32 = mybir.dt.float32
F16 = mybir.dt.float16
BF16 = mybir.dt.bfloat16
I32 = mybir.dt.int32
RMAX = bass.bass_isa.ReduceOp.max

P = 128
EPS = 1e-5

NF4 = [-1.0, -0.6961928009986877, -0.5250730514526367, -0.39491748809814453, -0.28444138169288635,
       -0.18477343022823334, -0.09105003625154495, 0.0, 0.07958029955625534, 0.16093020141124725,
       0.24611230194568634, 0.33791524171829224, 0.44070982933044434, 0.5626170039176941, 0.7229568362236023, 1.0]


def nf4_lines():
    f = np.float32

    def near(v, n):
        v = f(v)
        out, up, down = [v], v, v
        for _ in range(n):
            up, down = np.nextafter(up, f(9)), np.nextafter(down, f(-9))
            out += [up, down]
        return out

    def line(k, sign):
        v0, v1 = f(sign * NF4[k]), f(sign * NF4[k + 1])
        slope = float(v1) - float(v0)
        offset = float(v0) - slope * (k - 7)
        for a in near(slope, 8):
            for b in near(offset, 24):
                if (f(np.float64(a) * (k - 7) + np.float64(b)) == v0
                        and f(np.float64(a) * (k - 6) + np.float64(b)) == v1):
                    return float(a), float(b)
        raise AssertionError(k)

    return [line(k, 1.0) for k in (8, 10, 12, 14)], [(float(f(NF4[6])), 0.0)] + [line(k, -1.0) for k in (4, 2, 0)]


def build(nc, x, gate_codes, gate_scales, up_codes, up_scales, down_codes, down_scales, out):
    NB, C, H = x.shape
    I = gate_codes.shape[0]
    QB = 64
    NQ = C // P
    CH = NB * P
    KT = H // P
    FT = I // P
    REST = I - FT * P
    NT = FT + 1
    HALF = H // 2
    GB = H // QB
    DB = I // QB
    NU = 3 * FT + 2
    assert REST == QB and NB == 4 and KT == 8 and NQ == 8 and FT % 2 == 1

    XS, WS = 10, 8
    IS = 7

    pos_lines, neg_lines = nf4_lines()

    inter_scr = nc.dram_tensor("inter_scr", [NQ, NB, P, 2, NT * P], F16, kind="Internal").ap()
    wd_scr = nc.dram_tensor("wd_scr", [2, P, NT, 2, HALF], F16, kind="Internal").ap()
    prob_scr_t = nc.dram_tensor("prob_scr", [17, H], F32, kind="Internal")
    prob_scr = prob_scr_t.ap()

    with ExitStack() as ctx:
        def sb(name, shape, dt):
            return ctx.enter_context(nc.sbuf_tensor(name, shape, dt))

        def sem(name):
            return ctx.enter_context(nc.semaphore(name))

        big = sb("big", [P, NQ * 2 * KT * CH], F16)
        XT = big[:, :].rearrange("p (q s k t) -> p q s k t", q=NQ, s=2, k=KT)
        ARENA_KB = 68
        arena = sb("arena", [P, ARENA_KB * 256], F32)

        def carve(kb, size_kb, dt=F32):
            v = arena[:, int(kb * 256):int((kb + size_kb) * 256)]
            return v if dt == F32 else v.bitcast(dt)

        codes = carve(0, 4, I32)
        u_sb = carve(4, 4)
        acc_p = carve(8, 4)
        acc_n = carve(12, 4)
        ring = [carve(16, 4), carve(20, 4)]
        w_f = carve(24, 4)
        w_hl = carve(28, 4, F16).rearrange("p (s j) -> p s j", s=2)
        w_t = carve(32, 16, F16).rearrange("p (b g s k m) -> p b g s k m", b=2, g=2, s=2, k=KT)
        wd_stage32 = carve(48, 4)
        wd_stage = wd_stage32.bitcast(F16).rearrange("p (s j) -> p s j", s=2)
        xf = carve(52, 4)
        sil = [carve(56, 2), carve(58, 2)]
        inter_f = [carve(60, 2), carve(62, 2)]
        inter_hl = [carve(64, 2, F16).rearrange("p (s t) -> p s t", s=2),
                    carve(66, 2, F16).rearrange("p (s t) -> p s t", s=2)]
        x_wait = XT[:, NQ - 1, :, :, :].rearrange("p s k t -> p (s k t)").bitcast(F32).rearrange("p (n h) -> p n h", n=NB)
        prob_t = xf[0:17, :]

        wd_sb = big[:, 0:2 * NT * 2 * HALF].rearrange("p (e k s h) -> p e k s h", e=2, k=NT, s=2)
        pb0 = 2 * NT * 2 * HALF
        prob_b = big[:, pb0:pb0 + 2 * 16 * HALF].bitcast(F32).rearrange("p (j h) -> p j h", j=16)
        it_sb = [carve(0, 11, F16).rearrange("p (s k t) -> p s k t", s=2, k=NT),
                 carve(11, 11, F16).rearrange("p (s k t) -> p s k t", s=2, k=NT)]
        x2_at = pb0 + 2 * 16 * HALF
        x2 = [big[:, x2_at:x2_at + 2 * NB * HALF].bitcast(F32).rearrange("p (n h) -> p n h", n=NB),
              carve(32, 8).rearrange("p (n h) -> p n h", n=NB)]
        xn2 = carve(22, 8).rearrange("p (n h) -> p n h", n=NB)
        prod = carve(30, 2)
        msg = carve(40, 2)
        ffn = carve(42, 2)
        gate2 = carve(44, 2)
        sg = [carve(46, 2), carve(52, 2)]
        e_b = carve(48, 4)
        o_sb = [carve(56, 2), carve(58, 2)]

        s_g = sb("s_g", [P, NT, GB], F32)
        s_u = sb("s_u", [P, FT, GB], F32)
        s_d = sb("s_d", [P, KT, DB], F32)
        mx = sb("mx", [P, 2 * NT + KT], F32)
        inv = sb("inv", [P, 2 * NT + KT], F32)
        gu_prod = sb("gu_prod", [P, NT], F32)
        f_part = sb("f_part", [P, 1], F32)
        f_all = sb("f_all", [P, 1], F32)
        f_inv = sb("f_inv", [P, 1], F32)
        gate_back = sb("gate_back", [P, NT], F32)
        up_back = sb("up_back", [P, NT], F32)
        st = sb("st", [P, 2, 12], F32)
        mvt = sb("mvt", [P, 2, 2], F32)
        mean = sb("mean", [P, NQ * NB], F32)
        rstd = sb("rstd", [P, NQ * NB], F32)
        y = sb("y", [P, 10], F32)
        eps_t = sb("eps_t", [P, 1], F32)
        junk_v = sb("junk_v", [P, 2 * P], BF16)
        junk_a = sb("junk_a", [P, 2 * P], BF16)
        part = sb("part", [P, 10, 4], F32)
        pair = sb("pair", [P, KT, 10], F32)
        sc = sb("sc", [P, KT, 17], F32)
        mxs = sb("mxs", [P, KT, 4], F32)
        zero = sb("zero", [P, 1], F32)
        gb_cur = sb("gb_cur", [P, 2], F32)
        id32 = sb("id32", [P, P], F32)
        id16 = sb("id16", [P, P], F16)

        ps = ctx.enter_context(nc.psum_tensor("ps", [P, 8, 512], F32))
        tp = [ps[:, 4, :].bitcast(F16), ps[:, 5, :].bitcast(F16)]
        xp = [ps[:, 6 + h, :].rearrange("p (k t) -> p k t", t=P) for h in (0, 1)]

        scales_in = sem("scales_in")
        idents = sem("idents")
        consts = sem("consts")
        prep = sem("prep")
        f_red = sem("f_red")
        code_in = sem("code_in")
        u_made = sem("u_made")
        lines = sem("lines")
        max_done = sem("max_done")
        v_made = sem("v_made")
        w_made = sem("w_made")
        hilo_made = sem("hilo_made")
        tp_done = sem("tp_done")
        tp_evac = sem("tp_evac")
        wd_out = sem("wd_out")
        x_in = [sem(f"x_in{r}") for r in range(4)]
        bn_done = sem("bn_done")
        mv_done = sem("mv_done")
        root = sem("root")
        newton = sem("newton")
        rstd_made = sem("rstd_made")
        xn_ready = sem("xn_ready")
        xt_done = sem("xt_done")
        x_hi = sem("x_hi")
        x_lo = sem("x_lo")
        g_done = sem("g_done")
        up_done = sem("up_done")
        silu_done = sem("silu_done")
        inter_made = sem("inter_made")
        ihl_made = sem("ihl_made")
        inter_out = [sem("inter_out0"), sem("inter_out1")]
        xf_made = sem("xf_made")
        ttr_done = sem("ttr_done")
        sq_done = sem("sq_done")
        pair_made = sem("pair_made")
        gb_made = sem("gb_made")
        soft = sem("soft")
        soft2 = sem("soft2")
        expd = sem("expd")
        pt_done = sem("pt_done")
        pt_evac = sem("pt_evac")
        prob_out = sem("prob_out")
        wd_in = [sem(f"wd_in{r}") for r in range(4)]
        pb_in = sem("pb_in")
        e_in = sem("e_in")
        it_in = [sem("it_in0"), sem("it_in1")]
        x2_in = [sem("x2_in0"), sem("x2_in1")]
        xn2_made = sem("xn2_made")
        y_done = sem("y_done")
        msg_step = sem("msg_step")
        ffn_made = sem("ffn_made")
        g2_made = sem("g2_made")
        sg_made = sem("sg_made")
        o_made = sem("o_made")
        o_out = [sem("o_out0"), sem("o_out1")]

        OPENING = [("gate", 0), ("up", 0), ("gate", 1), ("up", 1), ("down", 0), ("down", 1), ("gate", 2), ("up", 2)]
        NBATCH = NQ * NB // 2

        def opening_half(k):
            return (4 + k // 4, k % 4 == 2) if k % 2 == 0 else None

        OPENING_TP = {3: 4, 7: 5, 14: 6}
        OPENING_EVAC = {5: 4, 9: 5, 15: 6}

        def x_slot(tt):
            return x_wait[:, tt % NB, :] if tt < (NQ - 1) * NB else [xf, wd_stage32][tt % 2]

        def x_parts(tt, h):
            q, n = tt // NB, tt % NB
            return [XT[:, q, s, 4 * h:4 * h + 4, n * P:(n + 1) * P] for s in (0, 1)]

        def unit(i, a):
            return 2 + 3 * i + a

        def kind_of(i, a):
            if isinstance(i, int) and i == FT - 1:
                return [("last", FT), ("down", FT - 1), ("down_last", FT)][a]
            return [("gate", i + 1), ("up", i + 1), ("down", i)][a]

        def attend_chunk(att, par, q):
            return None if att is None or q < 6 else 2 * par + q - 6

        def phase1(eng, tile):
            with eng.Fori(1, KT + 1) as pr:
                tile(pr * 2, 0, pr - 1)
                tile(pr * 2 + 1, 1, pr - 1)
            for i in range(2 * KT + 2, FT + 1):
                tile(i, i % 2, None)

        block = ctx.enter_context(nc.Block())

        @block.sync
        def _(sp):
            def load_codes(w, kind, t):
                if not (isinstance(w, int) and w == 0):
                    sp.wait_ge(u_made, w)
                if kind in ("gate", "up"):
                    src = gate_codes if kind == "gate" else up_codes
                    for a in (0, 64):
                        sp.dma_start(codes[a:a + 64, :], src[bass.ds(t * P + a, 64), :]).then_inc(code_in, 16)
                elif kind == "last":
                    sp.dma_start(codes[0:REST, :], gate_codes[FT * P:I, :]).then_inc(code_in, 16)
                    sp.dma_start(codes[REST:P, :], up_codes[FT * P:I, :]).then_inc(code_in, 16)
                else:
                    n = P if kind == "down" else REST
                    dst = codes[:, 0:KT * n].rearrange("p (t c) -> p t c", c=n)
                    src = down_codes.rearrange("(t p) i -> p t i", p=P)
                    for a in (4, 0):
                        sp.dma_start(dst[:, a:a + 4, :], src[:, a:a + 4, bass.ds(t * P, n)]).then_inc(code_in, 16)

            def load_x(tt):
                if tt >= NB and tt // NB < NQ - 1:
                    sp.wait_ge(xt_done, 2 * (tt - NB) + 2)
                elif tt >= (NQ - 1) * NB + 2:
                    sp.wait_ge(xt_done, 2 * (tt - 2) + 2)
                elif tt == (NQ - 1) * NB + 1:
                    sp.wait_ge(wd_out, 2 * 32)
                sp.dma_start(x_slot(tt), x[tt % NB, (tt // NB) * P:(tt // NB + 1) * P, :]).then_inc(x_in[tt % NB], 16)

            def store_inter(i, q, k, b2, last):
                sp.wait_ge(ihl_made, k * 2 + 2)
                rows = slice(REST, P) if last else slice(0, P)
                n_rows = REST if last else P
                for s in (1, 0):
                    sp.dma_start(
                        inter_scr[q, :, 0:n_rows, s, bass.ds(i * P, P)].rearrange("n p t -> p n t"),
                        inter_hl[b2][rows, s, :].rearrange("p (n t) -> p n t", n=NB),
                    ).then_inc(inter_out[b2], 16)

            def store_wd(w, t, kind):
                rows = P if kind == "down" else REST
                sp.wait_ge(tp_evac, w * 2 + 2)
                for hh in (0, 1):
                    sp.dma_start(wd_scr[hh, 0:rows, bass.ds(t, 1), :, :].rearrange("p o s h -> p (o s) h"),
                                 wd_stage[0:rows, :, hh * HALF:(hh + 1) * HALF]).then_inc(wd_out, 16)

            load_codes(0, *OPENING[0])
            sp.dma_start(s_g[:, 0:FT, :], gate_scales[0:FT * P, :].rearrange("(i p) b -> p i b", p=P)).then_inc(scales_in, 16)
            sp.dma_start(s_g[0:REST, FT, :], gate_scales[FT * P:I, :]).then_inc(scales_in, 16)
            sp.dma_start(s_g[REST:P, FT, :], up_scales[FT * P:I, :]).then_inc(scales_in, 16)
            sp.dma_start(s_u[:, :, :], up_scales[0:FT * P, :].rearrange("(i p) b -> p i b", p=P)).then_inc(scales_in, 16)
            sp.dma_start(s_d[:, :, :], down_scales.rearrange("(t p) b -> p t b", p=P)).then_inc(scales_in, 16)
            load_x(0)
            load_x(1)
            load_codes(1, *OPENING[1])
            load_x(2)
            load_x(3)
            load_codes(2, *OPENING[2])
            load_x(4)
            load_x(5)
            load_codes(3, *OPENING[3])
            load_x(6)
            load_x(7)
            load_codes(4, *OPENING[4])
            for k in range(16):
                b = k + 4 if k < 11 else k + 3
                if k != 11 and b < NBATCH:
                    load_x(2 * b)
                    load_x(2 * b + 1)
                if k in OPENING_EVAC and OPENING[OPENING_EVAC[k]][0] == "down":
                    store_wd(OPENING_EVAC[k], OPENING[OPENING_EVAC[k]][1], "down")
                h = opening_half(k)
                if h and h[1]:
                    w = h[0] + 1
                    load_codes(w, *(OPENING[w] if w < 8 else kind_of(2, 0)))
                store_inter(k % 2, k // 2, k, k % 2, False)

            def tile(i, par, att):
                last = isinstance(i, int) and i == FT
                if last:
                    sp.wait_ge(tp_evac, 2 * NU)
                for q in range(NQ):
                    if not last and q == 1:
                        load_codes(unit(i, 1), *kind_of(i, 1))
                    if not last and q == 3:
                        load_codes(unit(i, 2), *kind_of(i, 2))
                    if not (isinstance(i, int) and i >= FT - 1) and q == 5:
                        nxt = i + 1
                        load_codes(unit(nxt, 0), *kind_of(nxt, 0))
                    if isinstance(i, int) and i == FT - 1 and q == 5:
                        store_wd(unit(i, 1), FT - 1, "down")
                    if not last and q == 7:
                        k, t = kind_of(i, 2)
                        store_wd(unit(i, 2), t, k)
                    store_inter(i, q, i * NQ + q, q % 2, last)
                    if isinstance(i, int) and i == FT - 2 and q == 7:
                        sp.wait_ge(pt_evac, 1)
                        sp.dma_start(prob_scr[:, :], prob_t).then_inc(prob_out, 16)
                    if last and q < 3:
                        load_wd(0, *pieces[q], q)
                    if last and q == 3:
                        sp.wait_ge(inter_out[0], 32 * (FT * NQ // 2 + 1))
                        load_inter(0, 0, 0)
                        load_inter(0, 0, 1)

            per = XT.shape[2] * XT.shape[3] * CH // (2 * HALF)
            pieces = [(0, per), (per, 2 * per), (2 * per, NT)]

            def load_wd(e, a, b, q=NQ - 1):
                assert (e * NT + b - 1) // per <= q
                if e == 0 and q == 0:
                    sp.wait_ge(wd_out, 32 * NT)
                sp.wait_ge(g_done, FT * NQ + q + 1)
                full = min(b, FT)
                done = wd_in[q] if e == 0 else wd_in[3]
                if full > a:
                    sp.dma_start(wd_sb[:, e, a:full, :, :].rearrange("p k s h -> p (k s h)"),
                                 wd_scr[e, :, a:full, :, :].rearrange("p k s h -> p (k s h)")).then_inc(done, 16)
                if b == NT:
                    sp.dma_start(wd_sb[0:REST, e, FT, :, :], wd_scr[e, 0:REST, FT, :, :]).then_inc(done, 16)
                    sp.dma_start(wd_sb[REST:P, e, FT, 0, :], wd_scr[e, 0:REST, FT, 0, :]).then_inc(done, 16)

            def load_inter(e, q, n):
                s = (e * NQ + q) * NB + n
                if not (isinstance(q, int) and s < 2):
                    sp.wait_ge(y_done, s - 1)
                dst = it_sb[n % 2]
                src = inter_scr[bass.ds(q, 1), n, :, :, :].rearrange("o p s c -> (o p) s c")
                sp.dma_start(dst[0:REST, :, FT, :], src[0:REST, :, FT * P:NT * P]).then_inc(it_in[n % 2], 16)
                sp.dma_start(dst[REST:P, 0, FT, :], src[0:REST, 1, FT * P:NT * P]).then_inc(it_in[n % 2], 16)
                sp.dma_start(dst[:, :, 0:FT, :].rearrange("p s k t -> p s (k t)"), src[:, :, 0:FT * P]).then_inc(it_in[n % 2], 16)

            phase1(sp, tile)

            sp.wait_ge(inter_out[0], 32 * NT * NQ // 2)
            sp.wait_ge(inter_out[1], 32 * NT * NQ // 2)
            sp.wait_ge(prob_out, 16)

            def load_x2(e, q, b):
                if not (isinstance(q, int) and e == 0 and q < 2):
                    sp.wait_ge(o_made, (e * NQ + q - 1) * NB)
                sp.dma_start(x2[b], x[:, bass.ds(q * P, P), e * HALF:(e + 1) * HALF].rearrange("n p h -> p n h")).then_inc(x2_in[b], 16)

            def load_prob(e):
                src = bass.AP(prob_scr_t, e * HALF, [[0, P], [H, 16], [1, HALF]])
                sp.dma_start(prob_b, src).then_inc(pb_in, 16)

            def store_out(e, q, n):
                s = (e * NQ + q) * NB + n
                sp.wait_ge(o_made, s + 1)
                sp.dma_start(out[n, bass.ds(q * P, P), e * HALF:(e + 1) * HALF], o_sb[n % 2]).then_inc(o_out[n % 2], 16)

            load_x2(0, 0, 0)
            load_prob(0)
            sp.dma_start(e_b, bass.AP(prob_scr_t, 16 * H, [[0, P], [1, H]])).then_inc(e_in, 16)

            def half(e, q, b, final=False, wd=False):
                en, qn = (e + 1, 0) if final else (e, q + 1)
                for n in range(NB):
                    if n == 0 and en < 2:
                        load_x2(en, qn, 1 - b)
                    if n < 2:
                        load_inter(e, q, n + 2)
                    elif en < 2:
                        load_inter(en, qn, n - 2)
                    if wd:
                        at = 3 * (q * NB + n)
                        load_wd(1, at, min(at + 3, NT)) if at < NT else None
                    store_out(e, q, n)

            for e in (0, 1):
                if e == 1:
                    sp.wait_ge(msg_step, 7 * NQ * NB)
                    load_prob(1)
                half(e, 0, 0, wd=e == 0)
                half(e, 1, 1, wd=e == 0)
                with sp.Fori(1, NQ // 2 - 1) as pr:
                    half(e, pr * 2, 0)
                    half(e, pr * 2 + 1, 1)
                half(e, NQ - 2, 0)
                half(e, NQ - 1, 1, final=True)
            for b in (0, 1):
                sp.wait_ge(o_out[b], 16 * NQ * NB)

        @block.gpsimd
        def _(pool):
            g = nc.gpsimd
            g.memset(id32[:], 0.0).then_inc(idents, 1)
            g.memset(zero[:, :], 0.0).then_inc(idents, 1)
            pool.wait_ge(idents, 2)
            g.affine_select(out=id32[:], in_=id32[:], compare_op=ALU.not_equal, fill=1.0, base=0,
                            pattern=[[-1, P]], channel_multiplier=1).then_inc(idents, 1)
            pool.wait_ge(idents, 3)
            g.tensor_copy(id16[:], id32[:]).then_inc(idents, 1)

            def hilo(w, n=1024):
                pool.wait_ge(w_made, w + 1)
                if not (isinstance(w, int) and w == 0):
                    pool.wait_ge(tp_done, w)
                g.tensor_tensor(w_hl[:, 0, 0:n], w_f[:, 0:n], zero[:, 0:1].to_broadcast([P, n]), ALU.add).then_inc(hilo_made, 1)
                pool.wait_ge(hilo_made, w * 2 + 1)
                g.tensor_tensor(w_hl[:, 1, 0:n], w_f[:, 0:n], w_hl[:, 0, 0:n], ALU.subtract).then_inc(hilo_made, 1)

            pool.wait_ge(prep, 10)
            g.partition_all_reduce(f_all[:, :], f_part[:, :], P, RMAX).then_inc(f_red, 1)
            for w in range(4):
                hilo(w)

            def split_inter(k, b2, uses, last):
                rows = slice(REST, P) if last else slice(0, P)
                pool.wait_ge(inter_made, k + 1)
                if not (isinstance(k, int) and k < 2):
                    pool.wait_ge(inter_out[b2], uses * 32)
                hi, lo = inter_hl[b2][rows, 0, :], inter_hl[b2][rows, 1, :]
                src = inter_f[b2][rows, :]
                g.tensor_tensor(hi, src, zero[rows, 0:1].to_broadcast([rows.stop - rows.start, CH]), ALU.add).then_inc(ihl_made, 1)
                pool.wait_ge(ihl_made, k * 2 + 1)
                g.tensor_tensor(lo, src, hi, ALU.subtract).then_inc(ihl_made, 1)

            def size(i, a):
                return KT * REST if kind_of(i, a)[0] == "down_last" else 1024

            def tile(i, par, att):
                last = isinstance(i, int) and i == FT
                for q in range(NQ):
                    if not last and q in (1, 3, 5):
                        a = q // 2
                        hilo(unit(i, a), size(i, a))
                    j = attend_chunk(att, par, q)
                    if j is not None:
                        c = att * 4 + j
                        if j == 0:
                            pool.wait_ge(pair_made, att + 1)
                        else:
                            pool.wait_ge(ttr_done, c * 6)
                            pool.wait_ge(sq_done, c * 4)
                        v = [XT[:, 2 * j:2 * j + 2, s, bass.ds(att, 1), :].rearrange("p q o t -> p q (o t)") for s in (0, 1)]
                        g.tensor_tensor(xf.rearrange("p (q t) -> p q t", q=2), v[0], v[1], ALU.add).then_inc(xf_made, 1)
                    k = i * NQ + q
                    if last and q == 0:
                        pool.wait_ge(ihl_made, k * 2)
                    split_inter(k, q % 2, i * 4 + q // 2, last)

            for k in range(16):
                split_inter(k, k % 2, k // 2, False)
                h = opening_half(k)
                if h and h[1]:
                    hilo(h[0])
            phase1(pool, tile)
            pool.wait_ge(ihl_made, NT * NQ * 2)

            def half(e, q, b):
                for n in range(NB):
                    s = (e * NQ + q) * NB + n
                    pool.wait_ge(sg_made, s + 1)
                    if not (isinstance(s, int) and s < 2):
                        pool.wait_ge(o_out[n % 2], (e * NQ + q) * 32 + (n // 2) * 16)
                    g.tensor_tensor(o_sb[n % 2], sg[n % 2], x2[b][:, n, :], ALU.add).then_inc(o_made, 1)

            for e in (0, 1):
                half(e, 0, 0)
                half(e, 1, 1)
                with pool.Fori(1, NQ // 2) as pr:
                    half(e, pr * 2, 0)
                    half(e, pr * 2 + 1, 1)

        @block.scalar
        def _(act):
            a_ = nc.scalar

            def line_set(w, second, n=1024):
                first = isinstance(w, int) and w == 0
                for j, (slope, offset) in enumerate(neg_lines if second else pos_lines):
                    c = (3 if second else 0) + j - 1
                    if j == 0:
                        if not second:
                            act.wait_ge(u_made, w + 1)
                            if not first:
                                act.wait_ge(w_made, w)
                        dst = acc_n if second else acc_p
                    else:
                        if c >= 2:
                            act.wait_ge(max_done, w * 6 + c - 1)
                        dst = ring[c % 2]
                    if second and j == 0:
                        a_.activation(dst[:, 0:n], u_sb[:, 0:n], ACT.Relu, scale=slope).then_inc(lines, 1)
                    else:
                        a_.activation(dst[:, 0:n], u_sb[:, 0:n], ACT.Copy, bias=offset, scale=slope).then_inc(lines, 1)

            def x_root(b):
                act.wait_ge(mv_done, b * 2 + 2)
                if b:
                    act.wait_ge(newton, b * 5)
                a_.activation(y[:, 0:2], mvt[:, :, 1], ACT.Sqrt, bias=eps_t[:, 0:1], scale=2.0 ** (-2 * XS)).then_inc(root, 1)

            def x_hi_part(tt):
                for h in (0, 1):
                    act.wait_ge(xt_done, 2 * tt + h + 1)
                    a_.activation(x_parts(tt, h)[0], xp[h], ACT.Copy).then_inc(x_hi, 1)

            def silu(k, b2, last):
                act.wait_ge(g_done, k + 1)
                if not (isinstance(k, int) and k < 2):
                    act.wait_ge(inter_made, k - 1)
                src = ps[0:REST, b2, :] if last else ps[:, b2, :]
                dst = sil[b2][REST:P, :] if last else sil[b2]
                return src, dst

            line_set(0, False)
            line_set(0, True)
            act.wait_ge(consts, 1)
            x_root(0)
            line_set(1, False)
            line_set(1, True)
            x_hi_part(0)
            x_hi_part(1)
            x_root(1)
            x_hi_part(2)
            x_hi_part(3)
            line_set(2, False)
            line_set(2, True)
            x_root(2)
            line_set(3, False)
            line_set(3, True)
            x_hi_part(4)
            x_hi_part(5)
            act.wait_ge(gb_made, 2)
            src, dst = silu(0, 0, False)
            a_.activation(dst, src, ACT.Silu, scale=gb_cur[:, 0:1]).then_inc(silu_done, 1)
            x_root(3)
            x_root(4)
            x_hi_part(6)
            x_hi_part(7)
            line_set(4, False)
            src, dst = silu(1, 1, False)
            a_.activation(dst, src, ACT.Silu, scale=gb_cur[:, 1:2]).then_inc(silu_done, 1)
            for k in range(2, 16):
                b = k + 2
                if b < NBATCH:
                    x_hi_part(2 * b)
                if b + 1 < NBATCH:
                    x_root(b + 1)
                h = opening_half(k)
                if h:
                    line_set(*h)
                if b < NBATCH:
                    x_hi_part(2 * b + 1)
                src, dst = silu(k, k % 2, False)
                a_.activation(dst, src, ACT.Silu, scale=gb_cur[:, k % 2:k % 2 + 1]).then_inc(silu_done, 1)

            def tile(i, par, att):
                last = isinstance(i, int) and i == FT
                for q in range(NQ):
                    if not last and q < 6:
                        a = q // 2
                        n = KT * REST if kind_of(i, a)[0] == "down_last" else 1024
                        line_set(unit(i, a), q % 2 == 1, n)
                    j = attend_chunk(att, par, q)
                    if j is not None:
                        act.wait_ge(xf_made, att * 4 + j + 1)
                        if j == 0:
                            act.wait_ge(pair_made, att + 1)
                        v = xf.rearrange("p (q n t) -> p q n t", q=2, n=NB)
                        for n in range(NB):
                            at = [0, 4, 7, 9][n]
                            if n:
                                act.wait_ge(sq_done, (att * 4 + j) * 4 + n)
                            a_.activation(junk_a[:, :].rearrange("p (q t) -> p q t", q=2), v[:, :, n, :], ACT.Square,
                                                accum_out=part[:, at, j:j + 1]).then_inc(sq_done, 1)
                    if isinstance(i, int) and i == FT - 3 and q == 6:
                        act.wait_ge(soft2, 2 * NB)
                        a_.activation(sc[:, :, 0:16], sc[:, :, 0:16], ACT.Exp, scale=2.0 ** (-2 * XS) / float(H) ** 0.5).then_inc(expd, 1)
                    src, dst = silu(i * NQ + q, q % 2, last)
                    scale = gb_cur[0:REST, par:par + 1] if last else gb_cur[:, par:par + 1]
                    if q == 0:
                        act.wait_ge(gb_made, i + 1)
                    a_.activation(dst, src, ACT.Silu, scale=scale).then_inc(silu_done, 1)

            phase1(act, tile)

            def half(e, q, b):
                for n in range(NB):
                    s = (e * NQ + q) * NB + n
                    act.wait_ge(ffn_made, s + 1)
                    if not (isinstance(s, int) and s < 1):
                        act.wait_ge(sg_made, s)
                    a_.activation(gate2, ffn, ACT.Silu).then_inc(g2_made, 1)

            for e in (0, 1):
                half(e, 0, 0)
                half(e, 1, 1)
                with act.Fori(1, NQ // 2) as pr:
                    half(e, pr * 2, 0)
                    half(e, pr * 2 + 1, 1)

        @block.vector
        def _(dve):
            v_ = nc.vector
            v_.memset(part[:, :, :], 0.0).then_inc(pair_made, 1)
            v_.memset(eps_t[:, :], EPS * 2.0 ** (-2 * XS)).then_inc(consts, 1)

            def shift(w, n=1024):
                dve.wait_ge(code_in, w * 32 + 32)
                if not (isinstance(w, int) and w == 0):
                    dve.wait_ge(lines, w * 8)
                v_.tensor_scalar(u_sb[:, 0:n], codes[:, 0:n], -7.0, None, ALU.add).then_inc(u_made, 1)

            def maxima(w, second, n=1024):
                acc = acc_n if second else acc_p
                for j in (1, 2, 3):
                    c = (3 if second else 0) + j - 1
                    dve.wait_ge(lines, w * 8 + (4 if second else 0) + j + 1)
                    if j > 1:
                        dve.wait_ge(max_done, w * 6 + c)
                    v_.tensor_tensor(acc[:, 0:n], acc[:, 0:n], ring[c % 2][:, 0:n], ALU.max).then_inc(max_done, 1)

            def dequant(w, kind, t, n=1024):
                dve.wait_ge(max_done, w * 6 + 6)
                v_.scalar_tensor_tensor(acc_p[:, 0:n], acc_p[:, 0:n], 0.0, acc_n[:, 0:n], ALU.max, ALU.subtract).then_inc(v_made, 1)
                dve.wait_ge(v_made, w + 1)
                if not (isinstance(w, int) and w == 0):
                    dve.wait_ge(hilo_made, w * 2)
                if kind in ("gate", "up", "last"):
                    tab = s_u if kind == "up" else s_g
                    s = tab[:, bass.ds(t, 1), :].rearrange("p o b -> p (o b)")
                    shape, split = [P, GB, QB], "p (b c) -> p b c"
                    v_.tensor_tensor(w_f[:, :].rearrange(split, c=QB), acc_p[:, :].rearrange(split, c=QB),
                                     s.unsqueeze(2).to_broadcast(shape), ALU.mult).then_inc(w_made, 1)
                else:
                    nb = n // KT // QB
                    for b in range(nb):
                        s = s_d[:, :, bass.ds(t * 2 + b, 1)]
                        d = w_f[:, 0:n].rearrange("p (t b c) -> p t b c", t=KT, c=QB)[:, :, b, :]
                        a = acc_p[:, 0:n].rearrange("p (t b c) -> p t b c", t=KT, c=QB)[:, :, b, :]
                        ins = v_.tensor_tensor(d, a, s.to_broadcast([P, KT, QB]), ALU.mult)
                    ins.then_inc(w_made, 1)

            def evacuate(w, kind, par, d=None):
                dve.wait_ge(tp_done, w + 1)
                if kind in ("gate", "up", "last"):
                    gu = 1 if kind == "up" else 0
                    for s in (0, 1):
                        v_.tensor_copy(w_t[:, par, gu, s, :, :].rearrange("p k m -> p (k m)"), tp[s]).then_inc(tp_evac, 1)
                else:
                    if not (isinstance(d, int) and d == 0):
                        dve.wait_ge(wd_out, d * 32)
                    rows = P if kind == "down" else REST
                    for s in (0, 1):
                        v_.tensor_copy(wd_stage[0:rows, s, :], tp[s][0:rows, :]).then_inc(tp_evac, 1)

            def x_norm(b):
                for j in (0, 1):
                    tt = 2 * b + j
                    dve.wait_ge(x_in[tt % NB], (tt // NB) * 16 + 16)
                    for m in (0, 1):
                        v_.bn_stats(st[:, j, 6 * m:6 * m + 6], x_slot(tt)[:, m * 512:(m + 1) * 512]).then_inc(bn_done, 1)
                if b:
                    dve.wait_ge(xn_ready, 2 * b)
                for j in (0, 1):
                    dve.wait_ge(bn_done, b * 4 + 2 * j + 2)
                    v_.bn_aggr(mvt[:, j, :], st[:, j, :]).then_inc(mv_done, 1)
                dve.wait_ge(mv_done, b * 2 + 2)
                v_.tensor_scalar(y[:, 2:4], mvt[:, :, 1], EPS, 2.0 ** (-2 * XS), ALU.add, ALU.mult).then_inc(newton, 1)
                dve.wait_ge(root, b + 1)
                v_.reciprocal(y[:, 4:6], y[:, 0:2]).then_inc(newton, 1)
                dve.wait_ge(newton, b * 5 + 2)
                v_.tensor_tensor(y[:, 4:6], y[:, 4:6], y[:, 2:4], ALU.mult).then_inc(newton, 1)
                dve.wait_ge(newton, b * 5 + 3)
                v_.tensor_tensor(y[:, 6:8], y[:, 4:6], y[:, 0:2], ALU.add).then_inc(newton, 1)
                dve.wait_ge(newton, b * 5 + 4)
                v_.tensor_scalar(y[:, 6:8], y[:, 6:8], 0.5, None, ALU.mult).then_inc(newton, 1)
                dve.wait_ge(newton, b * 5 + 5)
                v_.reciprocal(rstd[:, 2 * b:2 * b + 2], y[:, 6:8]).then_inc(rstd_made, 1)
                v_.tensor_scalar(mean[:, 2 * b:2 * b + 2], mvt[:, :, 0], 1.0, None, ALU.mult)
                dve.wait_ge(rstd_made, b + 1)
                for j in (0, 1):
                    tt = 2 * b + j
                    v_.tensor_scalar(x_slot(tt), x_slot(tt), mvt[:, j, 0:1], rstd[:, tt:tt + 1],
                                     ALU.subtract, ALU.mult).then_inc(xn_ready, 1)

            def x_lo_part(tt):
                for h in (0, 1):
                    dve.wait_ge(x_hi, 2 * tt + h + 1)
                    hi, lo = x_parts(tt, h)
                    v_.tensor_tensor(lo, xp[h], hi, ALU.subtract).then_inc(x_lo, 1)

            def gated(k, b2, i, last):
                rows = slice(REST, P) if last else slice(0, P)
                dve.wait_ge(silu_done, k + 1)
                dve.wait_ge(g_done if last else up_done, k + 1)
                if not (isinstance(k, int) and k < 2):
                    dve.wait_ge(ihl_made, (k - 1) * 2)
                src = ps[rows, b2, :] if last else ps[:, 2 + b2, :]
                v_.scalar_tensor_tensor(inter_f[b2][rows, :], src, up_back[rows, bass.ds(i, 1)],
                                        sil[b2][rows, :], ALU.mult, ALU.mult).then_inc(inter_made, 1)

            shift(0)
            maxima(0, False)
            maxima(0, True)

            steps = [0]

            def step(ins, wait=True):
                ins.then_inc(prep, 1)
                steps[0] += 1
                if wait:
                    dve.wait_ge(prep, steps[0])

            dve.wait_ge(scales_in, 16 * 5)
            step(v_.tensor_reduce(mx[:, 0:NT], s_g[:, :, :], AX.X, ALU.max, apply_absolute_value=True), False)
            step(v_.tensor_reduce(mx[:, NT:NT + FT], s_u[:, :, :], AX.X, ALU.max, apply_absolute_value=True), False)
            step(v_.tensor_reduce(mx[:, 2 * NT:], s_d[:, :, :], AX.X, ALU.max, apply_absolute_value=True))
            step(v_.tensor_copy(mx[:, 2 * NT - 1:2 * NT], mx[:, NT - 1:NT]))
            step(v_.tensor_scalar(mx[:, :], mx[:, :], 2.0 ** -60, None, ALU.max))
            mi = mx[:, :].bitcast(I32)
            step(v_.tensor_scalar(mi, mi, 0x7F800000, None, ALU.bitwise_and))
            step(v_.reciprocal(inv[:, :], mx[:, :]))
            step(v_.tensor_scalar(inv[:, :], inv[:, :], 2.0 ** WS, None, ALU.mult))
            step(v_.tensor_tensor(gu_prod[:, :], mx[:, 0:NT], mx[:, NT:2 * NT], ALU.mult))
            step(v_.tensor_reduce(f_part[:, :], gu_prod[:, :], AX.X, ALU.max))
            step(v_.tensor_tensor(s_g[:, :, :], s_g[:, :, :], inv[:, 0:NT].unsqueeze(2).to_broadcast([P, NT, GB]), ALU.mult), False)
            step(v_.tensor_tensor(s_u[:, :, :], s_u[:, :, :], inv[:, NT:NT + FT].unsqueeze(2).to_broadcast([P, FT, GB]), ALU.mult), False)
            step(v_.tensor_tensor(s_d[:, :, :], s_d[:, :, :], inv[:, 2 * NT:].unsqueeze(2).to_broadcast([P, KT, DB]), ALU.mult), False)
            step(v_.tensor_scalar(gate_back[:, :], mx[:, 0:NT], 2.0 ** (-XS - WS), None, ALU.mult))
            dve.wait_ge(f_red, 1)
            step(v_.reciprocal(f_inv[:, :], f_all[:, :]))
            step(v_.tensor_scalar(up_back[:, :], mx[:, NT:2 * NT], f_inv[:, 0:1], 2.0 ** (-XS - WS - IS), ALU.mult, ALU.mult), False)
            step(v_.tensor_scalar(sc[:, :, 16:17].rearrange("p t o -> p (t o)"), mx[:, 2 * NT:], f_all[:, 0:1], 2.0 ** (IS - WS), ALU.mult, ALU.mult))
            for t in (0, 1):
                v_.tensor_scalar(gb_cur[:, t:t + 1], gate_back[:, t:t + 1], 1.0, None, ALU.mult).then_inc(gb_made, 1)

            shift(1)
            dequant(0, *OPENING[0])
            x_norm(0)
            maxima(1, False)
            evacuate(0, "gate", 0)
            maxima(1, True)
            x_lo_part(0)
            x_lo_part(1)
            shift(2)
            dequant(1, *OPENING[1])
            x_norm(1)
            evacuate(1, "up", 0)
            x_lo_part(2)
            x_lo_part(3)
            maxima(2, False)
            maxima(2, True)
            shift(3)
            dequant(2, *OPENING[2])
            x_norm(2)
            maxima(3, False)
            evacuate(2, "gate", 1)
            maxima(3, True)
            x_lo_part(4)
            x_lo_part(5)
            shift(4)
            dequant(3, *OPENING[3])
            gated(0, 0, 0, False)
            x_norm(3)
            evacuate(3, "up", 1)
            x_norm(4)
            x_lo_part(6)
            x_lo_part(7)
            maxima(4, False)
            gated(1, 1, 1, False)
            for k in range(2, 16):
                b = k + 2
                if k in OPENING_EVAC:
                    w = OPENING_EVAC[k]
                    kind, t = OPENING[w]
                    evacuate(w, kind, 0, t if kind == "down" else None)
                if b < NBATCH:
                    x_lo_part(2 * b)
                if b + 1 < NBATCH:
                    x_norm(b + 1)
                h = opening_half(k)
                if h:
                    maxima(*h)
                if b < NBATCH:
                    x_lo_part(2 * b + 1)
                if h and h[1]:
                    shift(h[0] + 1)
                    dequant(h[0], *OPENING[h[0]])
                if k == 15:
                    evacuate(7, "up", 0)
                gated(k, k % 2, k % 2, False)
                if k == 14:
                    v_.tensor_scalar(gb_cur[:, 0:1], gate_back[:, 2:3], 1.0, None, ALU.mult).then_inc(gb_made, 1)

            PAIRS = [(n, m) for n in range(NB) for m in range(n, NB)]

            def softmax():
                c = [0]

                def st_(ins):
                    c[0] += 1
                    ins.then_inc(soft, 1)
                    dve.wait_ge(soft, c[0])

                dve.wait_ge(pair_made, KT + 1)
                at = 0
                for n in range(NB):
                    k = NB - n
                    st_(v_.tensor_copy(sc[:, :, 4 * n + n:4 * n + 4], pair[:, :, at:at + k]))
                    if k > 1:
                        st_(v_.tensor_copy(sc[:, :, 4 * (n + 1) + n:4 * (NB - 1) + n + 1:4], pair[:, :, at + 1:at + k]))
                    at += k
                s3 = [sc[:, :, 4 * n:4 * n + 4] for n in range(NB)]
                for n in range(NB):
                    v_.tensor_reduce(mxs[:, :, n:n + 1], s3[n], AX.X, ALU.max).then_inc(soft2, 1)
                dve.wait_ge(soft2, NB)
                for n in range(NB):
                    v_.tensor_tensor(s3[n], s3[n], mxs[:, :, n:n + 1].to_broadcast([P, KT, NB]), ALU.subtract).then_inc(soft2, 1)
                dve.wait_ge(soft2, 2 * NB)

            def softmax_end():
                dve.wait_ge(expd, 1)
                s3 = [sc[:, :, 4 * n:4 * n + 4] for n in range(NB)]
                for n in range(NB):
                    v_.tensor_reduce(mxs[:, :, n:n + 1], s3[n], AX.X, ALU.add).then_inc(soft2, 1)
                dve.wait_ge(soft2, 3 * NB)
                v_.reciprocal(mxs[:, :, :], mxs[:, :, :]).then_inc(soft2, 1)
                dve.wait_ge(soft2, 3 * NB + 1)
                for n in range(NB):
                    v_.tensor_tensor(s3[n], s3[n], mxs[:, :, n:n + 1].to_broadcast([P, KT, NB]), ALU.mult).then_inc(soft2, 1)
                dve.wait_ge(soft2, 4 * NB + 1)
                diag = sc[:, :, 0:16:5]
                v_.tensor_scalar(diag, diag, 1.0, None, ALU.add).then_inc(soft2, 1)
                dve.wait_ge(soft2, 4 * NB + 2)
                v_.tensor_scalar(sc[:, :, 0:16], sc[:, :, 0:16], 2.0 ** -XS, None, ALU.mult).then_inc(soft2, 1)

            def tile(i, par, att):
                last = isinstance(i, int) and i == FT
                for q in range(NQ):
                    if not last and q < 6:
                        a = q // 2
                        kind, t = kind_of(i, a)
                        n = KT * REST if kind == "down_last" else 1024
                        maxima(unit(i, a), q % 2 == 1, n)
                        if q % 2:
                            if a < 2:
                                shift(unit(i, a + 1), KT * REST if kind_of(i, a + 1)[0] == "down_last" else 1024)
                            elif not (isinstance(i, int) and i == FT - 1):
                                shift(unit(i, 3))
                            dequant(unit(i, a), kind, t, n)
                    j = attend_chunk(att, par, q)
                    if j is not None:
                        dve.wait_ge(xf_made, att * 4 + j + 1)
                        xv = xf.rearrange("p (q n t) -> p q n t", q=2, n=NB)
                        done = 0
                        for at, (n, m) in enumerate(PAIRS):
                            if n != m:
                                if done:
                                    dve.wait_ge(ttr_done, (att * 4 + j) * 6 + done)
                                done += 1
                                v_.tensor_tensor_reduce(
                                    junk_v[:, :].rearrange("p (q t) -> p q t", q=2), xv[:, :, n, :], xv[:, :, m, :], 1.0, 0.0,
                                    ALU.mult, ALU.add, part[:, at, j:j + 1]).then_inc(ttr_done, 1)
                        if j == 3:
                            dve.wait_ge(ttr_done, att * 24 + 24)
                            dve.wait_ge(sq_done, att * 16 + 16)
                            v_.tensor_reduce(pair[:, bass.ds(att, 1), :].rearrange("p o c -> p (o c)"), part[:, :, :], AX.X, ALU.add).then_inc(pair_made, 1)
                    if isinstance(i, int) and i == FT - 3:
                        if q == 6:
                            softmax()
                        if q == 7:
                            softmax_end()
                    if isinstance(i, int) and i == FT - 2 and q == 6:
                        dve.wait_ge(pt_done, 1)
                        v_.tensor_copy(prob_t, ps[0:17, 6:8, :].rearrange("p b c -> p (b c)")).then_inc(pt_evac, 1)
                    if not last and q == 7:
                        v_.tensor_scalar(gb_cur[:, 1 - par:2 - par], gate_back[:, bass.ds(i + 1, 1)], 1.0, None, ALU.mult).then_inc(gb_made, 1)
                    if not last and q in (3, 5, 7):
                        a = q // 2 - 1
                        kind, t = kind_of(i, a)
                        d = None if kind not in ("down", "down_last") else t
                        evacuate(unit(i, a), kind, 1 - par, d)
                    gated(i * NQ + q, q % 2, i, last)

            phase1(dve, tile)

            dve.wait_ge(e_in, 16)

            def half(e, q, b):
                qq = e * NQ + q
                dve.wait_ge(x2_in[b], (qq // 2 if isinstance(qq, int) else pr_uses(e, q)) * 16 + 16)
                if not (isinstance(qq, int) and qq == 0):
                    dve.wait_ge(msg_step, qq * NB * 7)
                for m in range(NB):
                    v_.tensor_scalar(xn2[:, m, :], x2[b][:, m, :], mean[:, bass.ds(q * 4 + m, 1)],
                                     rstd[:, bass.ds(q * 4 + m, 1)], ALU.subtract, ALU.mult).then_inc(xn2_made, 1)
                for n in range(NB):
                    s = qq * NB + n
                    base = s * 7
                    if not (isinstance(s, int) and s == 0):
                        dve.wait_ge(sg_made, s)
                    for m in range(NB):
                        dve.wait_ge(xn2_made, qq * NB + m + 1)
                        if m >= 2:
                            dve.wait_ge(msg_step, base + 2 * m - 1)
                        v_.tensor_tensor(msg if m == 0 else prod, prob_b[:, 4 * n + m, :], xn2[:, m, :], ALU.mult).then_inc(msg_step, 1)
                        if m > 0:
                            dve.wait_ge(msg_step, base + 2 * m)
                            v_.tensor_tensor(msg, msg, prod, ALU.add).then_inc(msg_step, 1)
                    dve.wait_ge(y_done, s + 1)
                    if not (isinstance(s, int) and s == 0):
                        dve.wait_ge(g2_made, s)
                    v_.tensor_tensor(ffn, ps[:, 4 + n, :], e_b[:, e * HALF:(e + 1) * HALF], ALU.mult).then_inc(ffn_made, 1)
                    dve.wait_ge(g2_made, s + 1)
                    dve.wait_ge(msg_step, base + 7)
                    if not (isinstance(s, int) and s < 2):
                        dve.wait_ge(o_made, s - 1)
                    v_.tensor_tensor(sg[n % 2], msg, gate2, ALU.mult).then_inc(sg_made, 1)

            def pr_uses(e, q):
                raise AssertionError

            for e in (0, 1):
                dve.wait_ge(pb_in, 16 * (e + 1))
                half(e, 0, 0)
                half(e, 1, 1)
                with dve.Fori(1, NQ // 2) as pr:
                    pr_uses = lambda e, q, pr=pr: pr + e * (NQ // 2)
                    half(e, pr * 2, 0)
                    half(e, pr * 2 + 1, 1)

        @block.tensor
        def _(pe):
            t_ = nc.tensor
            pe.wait_ge(idents, 4)

            def transpose_unit(w, kind):
                pe.wait_ge(hilo_made, w * 2 + 2)
                if not (isinstance(w, int) and w == 0):
                    pe.wait_ge(tp_evac, w * 2)
                n = REST if kind == "down_last" else P
                for s in (0, 1):
                    for k in range(KT):
                        ins = t_.transpose(tp[s][0:n, k * P:(k + 1) * P], w_hl[:, s, k * n:(k + 1) * n], id16[:, :])
                ins.then_inc(tp_done, 1)

            def transpose_x(tt):
                pe.wait_ge(xn_ready, tt + 1)
                for h in (0, 1):
                    if tt:
                        pe.wait_ge(x_lo, 2 * tt + h - 1)
                    for k in range(4):
                        ins = t_.transpose(xp[h][:, k, :], x_slot(tt)[:, (4 * h + k) * P:(4 * h + k + 1) * P], id32[:, :])
                    ins.then_inc(xt_done, 1)

            TERMS = [(0, 0), (0, 1), (1, 0)]

            def product(bank, par, gu, q):
                for k in range(KT):
                    for a, b in TERMS:
                        ins = t_.matmul(ps[:, bank, :], w_t[:, par, gu, a, k, :], XT[:, q, b, k, :],
                                        start=(k == 0 and (a, b) == TERMS[0]), stop=(k == KT - 1 and (a, b) == TERMS[-1]))
                return ins

            def gate_product(k, q, b2, par, last):
                if not (isinstance(k, int) and k < 2):
                    pe.wait_ge(silu_done, k - 1)
                    if last:
                        pe.wait_ge(inter_made, k - 1)
                product(b2, par, 0, q).then_inc(g_done, 1)

            def up_product(k, q, b2, par):
                if not (isinstance(k, int) and k < 2):
                    pe.wait_ge(inter_made, k - 1)
                product(2 + b2, par, 1, q).then_inc(up_done, 1)

            transpose_unit(0, "gate")
            transpose_x(0)
            transpose_x(1)
            transpose_unit(1, "up")
            transpose_x(2)
            transpose_x(3)
            pe.wait_ge(x_lo, 2 * NB)
            for k in (0, 1):
                if k:
                    transpose_unit(2, "gate")
                    transpose_x(4)
                    transpose_x(5)
                pe.wait_ge(tp_evac, 4 * k + 2)
                gate_product(k, 0, k, k, False)
                if k:
                    transpose_unit(3, "up")
                pe.wait_ge(tp_evac, 4 * k + 4)
                up_product(k, 0, k, k)
            transpose_x(6)
            transpose_x(7)
            for k in range(2, 16):
                b = k + 2
                if b < NBATCH - 1:
                    transpose_x(2 * b)
                if k % 2 == 0:
                    pe.wait_ge(x_lo, 2 * NB * (k // 2 + 1))
                gate_product(k, k // 2, k % 2, k % 2, False)
                if b < NBATCH:
                    transpose_x(2 * b + 1 if b < NBATCH - 1 else 2 * b)
                if k == 15:
                    transpose_unit(7, "up")
                up_product(k, k // 2, k % 2, k % 2)
                if b == NBATCH - 1:
                    transpose_x(2 * b + 1)
                if k in OPENING_TP:
                    transpose_unit(OPENING_TP[k], OPENING[OPENING_TP[k]][0])

            def tile(i, par, att):
                last = isinstance(i, int) and i == FT
                for q in range(NQ):
                    if q == 0:
                        pe.wait_ge(tp_evac, 2 * unit(FT - 1, 0) + 2 if last else i * 6 + 4)
                    gate_product(i * NQ + q, q, q % 2, par, last)
                    if not last:
                        up_product(i * NQ + q, q, q % 2, par)
                        if q in (2, 4, 6):
                            a = q // 2 - 1
                            transpose_unit(unit(i, a), kind_of(i, a)[0])
                    if isinstance(i, int) and i == FT - 2 and q == 3:
                        pe.wait_ge(soft2, 4 * NB + 3)
                        for t in range(KT):
                            ins = t_.transpose(ps[0:17, 6 + t // 4, (t % 4) * P:(t % 4 + 1) * P], sc[:, t, :], id32[:, :])
                        ins.then_inc(pt_done, 1)

            phase1(pe, tile)

            pe.wait_ge(tp_evac, 2 * NU)

            def half(e, q, uses):
                for n in range(NB):
                    s = (e * NQ + q) * NB + n
                    pe.wait_ge(it_in[n % 2], (uses + n // 2) * 48 + 48)
                    if not (isinstance(s, int) and s < NB):
                        pe.wait_ge(ffn_made, s - NB + 1)
                    for k in range(FT):
                        if (e, n) == (0, 0) and isinstance(q, int) and k % KT == 0:
                            pe.wait_ge(wd_in[k // KT], 48 if k // KT == 2 else 16)
                        for a, b in TERMS:
                            t_.matmul(ps[:, 4 + n, :], it_sb[n % 2][:, a, k, :], wd_sb[:, e, k, b, :],
                                      start=(k == 0 and (a, b) == TERMS[0]), stop=False)
                    t_.matmul(ps[:, 4 + n, :], it_sb[n % 2][:, 0, FT, :], wd_sb[:, e, FT, 0, :], start=False, stop=False)
                    ins = t_.matmul(ps[:, 4 + n, :], it_sb[n % 2][0:REST, 0, FT, :], wd_sb[0:REST, e, FT, 1, :],
                                    start=False, stop=True)
                    ins.then_inc(y_done, 1)

            for e in (0, 1):
                if e == 1:
                    pe.wait_ge(wd_in[3], 9 * 16)
                half(e, 0, e * NQ * 2)
                with pe.Fori(1, NQ) as q:
                    half(e, q, q * 2 + e * NQ * 2)


_INS = ['L0_attn_x', 'L0_ffn_gate_codes', 'L0_ffn_gate_scales', 'L0_ffn_up_codes', 'L0_ffn_up_scales',
        'L0_ffn_down_codes', 'L0_ffn_down_scales']


def kernel(**inputs):
    import numpy as _np
    import concourse.bacc as _bacc
    from concourse import mybir as _mybir
    from concourse.bass_utils import run_bass_kernel_spmd as _run

    nc = _bacc.Bacc("TRN2", target_bir_lowering=False, num_devices=1)
    arrays, args = {}, []
    for name in _INS:
        a = _np.ascontiguousarray(inputs[name])
        arrays[f"in_{name}"] = a
        args.append(nc.dram_tensor(f"in_{name}", a.shape, _mybir.dt.from_np(a.dtype), kind="ExternalInput").ap())
    shape = arrays["in_L0_attn_x"].shape
    out = nc.dram_tensor("out_0", shape, _mybir.dt.float32, kind="ExternalOutput").ap()
    build(nc, *args, out)
    r = _run(nc, [arrays], core_ids=[0])
    return r.results[0]["out_0"]
```
